# Optimizing a Trainium2 kernel written in Bass

```python
import numpy as np
import jax
import jax.numpy as jnp

def _softmax(x, axis=-1):
    return jax.nn.softmax(x, axis=axis)

def _gelu(x):
    return jax.nn.gelu(x, approximate=True)

def _silu(x):
    return jax.nn.silu(x)

def _sigmoid(x):
    return jax.nn.sigmoid(x)

def _layernorm(x, axis=-1, eps=1e-05):
    m = jnp.mean(x, axis=axis, keepdims=True)
    v = jnp.var(x, axis=axis, keepdims=True)
    return (x - m) / jnp.sqrt(v + eps)

def _scatter_add(tgt, idx, src, axis=0):
    return tgt.at[idx].add(src)

def _segment_sum(src, seg, n):
    return jax.ops.segment_sum(src, seg, n)
kernel_name = 'mk_sandwich_d1_jaxref_r8_7b3f67'

def setup_inputs(seed: int=0):
    np.random.seed(seed)
    _w = jnp.asarray

    def _L0_attn_setup():
        import jax, jax.numpy as jnp
        import numpy as np
        B, S, D, H, HD = (2, 256, 128, 16, 64)
        key = jax.random.key(seed)
        ks = jax.random.split(key, 5)
        sc = 1.0 / np.sqrt(D)
        return {'x': jax.random.normal(ks[0], (B, S, D), jnp.float32), 'Wq': jax.random.normal(ks[1], (D, H, HD), jnp.float32) * sc, 'bq': jnp.zeros((H, HD), jnp.float32), 'Wk': jax.random.normal(ks[2], (D, H, HD), jnp.float32) * sc, 'bk': jnp.zeros((H, HD), jnp.float32), 'Wv': jax.random.normal(ks[3], (D, H, HD), jnp.float32) * sc, 'bv': jnp.zeros((H, HD), jnp.float32), 'Wo': jax.random.normal(ks[4], (H, HD, D), jnp.float32) * (1.0 / np.sqrt(H * HD)), 'bo': jnp.zeros((D,), jnp.float32)}
    _L0_attn_in = _L0_attn_setup()

    def _L0_ffn_setup():
        import jax, jax.numpy as jnp
        import numpy as np
        D_MODEL, D_FF, RANK = (128, 512, 32)
        B, S = (4, 512)
        key = jax.random.key(seed)
        ks = jax.random.split(key, 7)
        return {'x': jax.random.normal(ks[0], (B, S, D_MODEL), dtype=jnp.float32), 'U1': jax.random.normal(ks[1], (D_MODEL, RANK), dtype=jnp.float32) * 0.02, 'V1': jax.random.normal(ks[2], (RANK, D_FF), dtype=jnp.float32) * 0.02, 'b1': jnp.zeros((D_FF,), dtype=jnp.float32), 'U2': jax.random.normal(ks[3], (D_FF, RANK), dtype=jnp.float32) * 0.02, 'V2': jax.random.normal(ks[4], (RANK, D_MODEL), dtype=jnp.float32) * 0.02, 'b2': jnp.zeros((D_MODEL,), dtype=jnp.float32)}
    _L0_ffn_in = _L0_ffn_setup()
    _d = {'L0_attn_x': _L0_attn_in['x'], 'L0_attn_Wq': _L0_attn_in['Wq'], 'L0_attn_bq': _L0_attn_in['bq'], 'L0_attn_Wk': _L0_attn_in['Wk'], 'L0_attn_bk': _L0_attn_in['bk'], 'L0_attn_Wv': _L0_attn_in['Wv'], 'L0_attn_bv': _L0_attn_in['bv'], 'L0_attn_Wo': _L0_attn_in['Wo'], 'L0_attn_bo': _L0_attn_in['bo'], 'L0_ffn_U1': _L0_ffn_in['U1'], 'L0_ffn_V1': _L0_ffn_in['V1'], 'L0_ffn_b1': _L0_ffn_in['b1'], 'L0_ffn_U2': _L0_ffn_in['U2'], 'L0_ffn_V2': _L0_ffn_in['V2'], 'L0_ffn_b2': _L0_ffn_in['b2']}
    _x0 = _d['L0_attn_x']
    _d['L0_attn_x'] = jax.random.normal(jax.random.fold_in(jax.random.key(seed), 1), (2, 2048, 128), dtype=_x0.dtype)
    del _x0
    return _d

def reference(L0_attn_x, L0_attn_Wq, L0_attn_bq, L0_attn_Wk, L0_attn_bk, L0_attn_Wv, L0_attn_bv, L0_attn_Wo, L0_attn_bo, L0_ffn_U1, L0_ffn_V1, L0_ffn_b1, L0_ffn_U2, L0_ffn_V2, L0_ffn_b2):

    def _L0_attn_ref(x, Wq, bq, Wk, bk, Wv, bv, Wo, bo):
        import jax, jax.numpy as jnp
        import numpy as np
        B, S, D, H, HD = (2, 256, 128, 16, 64)
        q = jnp.einsum('bsd,dhk->bshk', x, Wq) + bq
        k = jnp.einsum('bsd,dhk->bshk', x, Wk) + bk
        v = jnp.einsum('bsd,dhk->bshk', x, Wv) + bv
        depth = q.shape[-1]
        q = q / jnp.sqrt(jnp.asarray(depth, q.dtype))
        attn = jnp.einsum('bqhd,bkhd->bhqk', q, k)
        attn = jax.nn.softmax(attn, axis=-1)
        out = jnp.einsum('bhqk,bkhd->bqhd', attn, v)
        return jnp.einsum('bqhd,hdm->bqm', out, Wo) + bo

    def _L0_ffn_ref(x, U1, V1, b1, U2, V2, b2):
        import jax, jax.numpy as jnp
        import numpy as np
        D_MODEL, D_FF, RANK = (128, 512, 32)
        B, S = (4, 512)
        P = jnp.einsum('bsd,dr->bsr', x, U1)
        H = jax.nn.gelu(jnp.einsum('bsr,rf->bsf', P, V1) + b1)
        Q = jnp.einsum('bsf,fr->bsr', H, U2)
        return jnp.einsum('bsr,rd->bsd', Q, V2) + b2
    x = L0_attn_x
    x = x + _layernorm(_L0_attn_ref(_layernorm(x, axis=-1), L0_attn_Wq, L0_attn_bq, L0_attn_Wk, L0_attn_bk, L0_attn_Wv, L0_attn_bv, L0_attn_Wo, L0_attn_bo), axis=-1)
    x = x + _layernorm(_L0_ffn_ref(_layernorm(x, axis=-1), L0_ffn_U1, L0_ffn_V1, L0_ffn_b1, L0_ffn_U2, L0_ffn_V2, L0_ffn_b2), axis=-1)
    return x

_drawn_inputs = setup_inputs


def setup_inputs(seed=0):
    import zlib

    import numpy as np

    out = dict(_drawn_inputs(seed))
    spreads = {'L0_attn_bq': (0.0, 0.269),
     'L0_attn_bk': (0.0, 0.8),
     'L0_attn_bv': (0.0, 0.1),
     'L0_attn_bo': (0.0, 0.1),
     'L0_ffn_b1': (0.0, 0.408),
     'L0_ffn_b2': (0.0, 0.1)}
    factors = {'L0_ffn_U1': 8.0, 'L0_ffn_V1': 8.0, 'L0_ffn_U2': 3.36, 'L0_ffn_V2': 2.795}
    for name, (base, spread) in spreads.items():
        noise = np.random.default_rng([zlib.crc32(name.encode()), seed]).standard_normal(out[name].shape)
        drawn = base * np.exp(spread * noise) if base else spread * noise
        out[name] = jnp.asarray(drawn.astype(out[name].dtype))
    for name, factor in factors.items():
        out[name] = (out[name] * factor).astype(out[name].dtype)
    return out
```

```python
import concourse.bass as bass
from concourse import mybir
from contextlib import ExitStack

F32 = mybir.dt.float32
F32R = mybir.dt.float32r
ALU = mybir.AluOpType
ACT = mybir.ActivationFunctionType
AX = mybir.AxisListType

P = 128
B, S, D = 2, 2048, 128
H, HD = 16, 64
FF, RANK = 512, 32
EPS = 1e-5
PAIRS = H // 2
T = S // P
CH = 512
NC = S // CH
TC = CH // P
STEPS = NC * T
PRING = 4
SCALE = float(HD) ** -0.5

SCORE_N = 2 * STEPS
PV_N = STEPS
MAXN = 2 * TC * NC * NC
SUM_N = NC * (T // 2 - 1)
KQ_N = 2 * NC
KQ_DMA_N = 6 * 16 * NC // 2
M_DMA_N = 2 * 16 * NC // 2

W_DMA_N = 6 * 16 // B
WO_DMA_N = 16 // B
UNIT_COUNTS = sorted({SCORE_N, PV_N, MAXN, SUM_N, KQ_N, KQ_DMA_N, M_DMA_N, NC, W_DMA_N, WO_DMA_N})

K_AT = [0, 1, 2, 3]
V_AT = [8, 12, 18, 20]
Q_AT = [4, 16, 30, 44]
PAIRS_OF_MAX = TC * NC * NC
MAX_FIRST = 6


def max_step(r):
    return MAX_FIRST + r * (STEPS - MAX_FIRST) // PAIRS_OF_MAX


M_LAG = 3
M_AT = [max_step(TC * NC * (c + 1) - 1) + M_LAG for c in range(NC)]
M_LATE = M_AT[-1] - STEPS


def prep_order():
    ops = [(K_AT[c], "K", c) for c in range(NC)] + [(V_AT[c], "V", c) for c in range(NC)]
    ops += [(Q_AT[c], "Q", c) for c in range(NC)] + [(M_AT[c], "M", c) for c in range(NC - 1)]
    return sorted(ops)


PREP = prep_order()


def build(nc, x, Wq, bq, Wk, bk, Wv, bv, Wo, bo, U1, V1, b1, U2, V2, b2, out):
    x_v = x.rearrange("b (t p) d -> p (b t) d", p=P)
    out_v = out.rearrange("b (t p) d -> p (b t) d", p=P)
    wq_v = Wq.rearrange("d (i h) k -> i d (h k)", h=2)
    wk_v = Wk.rearrange("d (i h) k -> i d (h k)", h=2)
    wv_v = Wv.rearrange("d (i h) k -> i d (h k)", h=2)
    wo_v = Wo.rearrange("(i h) k m -> i (h k) m", h=2)
    bq_v = bq.rearrange("(i h) k -> i (h k)", h=2)
    bk_v = bk.rearrange("(i h) k -> i (h k)", h=2)
    bv_v = bv.rearrange("(i h) k -> i (h k)", h=2)

    ctx = ExitStack()
    with ctx:
        def sb(name, shape, dt=F32):
            return ctx.enter_context(nc.sbuf_tensor(name, shape, dt))

        def sem(name):
            return ctx.enter_context(nc.semaphore(name))

        ident = sb("ident", [P, P])
        ones = sb("ones", [P, HD])
        xnT = sb("xnT", [P, B * S])
        y_acc = sb("y_acc", [P, B * T, D])
        w_qkv = sb("w_qkv", [P, 3, P])
        b_qk = sb("b_qk", [P, 2])
        b_v = sb("b_v", [P, P])
        w_o = sb("w_o", [P, D])
        k_dup = [sb(f"k_dup{b}", [P, 2, S], F32R) for b in range(B)]
        k_low = [sb(f"k_low{b}", [HD + 1, 2, S], F32R) for b in range(B)]
        q_split = sb("q_split", [P, 2, S], F32R)
        q_max = sb("q_max", [HD + 1, 2, S], F32R)
        v_sb = [sb(f"v_sb{b}", [P, T, P]) for b in range(B)]
        kq_f32 = sb("kq_f32", [P, 2, CH])
        k_hi = sb("k_hi", [P, 2, CH], F32R)
        k_lo = sb("k_lo", [P, 2, CH], F32R)
        q_hi = sb("q_hi", [P, 2, CH], F32R)
        q_lo = sb("q_lo", [P, 2, CH], F32R)
        probs = sb("probs", [P, PRING, 2, CH])
        sum_even = sb("sum_even", [P, 2, CH])
        sum_odd = sb("sum_odd", [P, 2, CH])
        sum_all = sb("sum_all", [P, 2, CH])
        denom = sb("denom", [P, CH])
        o_norm = sb("o_norm", [P, CH])
        max_part = sb("max_part", [P, 2, 2 * TC, NC])
        neg_max = sb("neg_max", [P, 2, 2 * TC])
        max_rows = sb("max_rows", [2 * TC, 2, P], F32R)
        ln_stats = sb("ln_stats", [P, 2, TC, 6])
        ln_mv = sb("ln_mv", [P, 2, TC, 2])
        ln_rstd = sb("ln_rstd", [P, 2, TC])
        ln_var = sb("ln_var", [P, 2, TC])
        minus_half = sb("minus_half", [P, TC])

        def bank(name):
            return ctx.enter_context(nc.psum_tensor(name, [P, CH], F32))

        score_ps = [bank(f"score_ps{h}") for h in range(2)]
        max_ps = [bank(f"max_ps{h}") for h in range(2)]
        o_ps = [bank(f"o_ps{n}") for n in range(2)]
        proj_ps = bank("proj_ps")
        tail_ps = bank("tail_ps")

        names = """half_ready eps_added const_ready x_in0 x_in1 stats_done mv_done rstd_done xn_done xnT_ps_ready xnT_done y_init
            w_in wo_in k_ps q_ps v_ps m_ps kq_evac kq_hi_done kq_split v_done
            m_evac k_dma0 k_dma1 q_dma0 q_dma1 m_dma0 m_dma1 ones_row
            score_ready exp_done pv_done sum_even_done sum_odd_done sum_all_done
            denom_ps_ready denom_done o_norm_done wo_ps_ready y_done max_ready max_done neg_max_done""".split()
        s = {n: sem(n) for n in names}
        k_dma, q_dma, m_dma = ([s[f"{n}_dma{j}"] for j in range(2)] for n in "kqm")

        class Pair:

            def __init__(self, eng, number, base, spare, shift=0):
                self.eng, self.number, self.base, self.spare, self.shift = eng, number, base, spare, shift

            def __add__(self, n):
                return Pair(self.eng, self.number, self.base, self.spare, self.shift + n)

            def __sub__(self, n):
                return self + -n

        def at(unit, per_unit, n):
            i, b = unit
            n += b * per_unit
            if isinstance(i, int):
                return i * B * per_unit + n
            n += i.shift * B * per_unit
            if n == 0:
                return i.base[per_unit]
            spare = i.spare.pop(0)
            i.spare.append(spare)
            i.eng.reg_add(spare, i.base[per_unit], n)
            return spare

        def number(i):
            return i if isinstance(i, int) else i.number + i.shift

        def is_first(unit):
            return isinstance(unit[0], int) and unit == (0, 0)

        def following(unit):
            i, b = unit
            return (i, 1) if b == 0 else (i + 1, 0)


        def proj_free(pe, v, kind, c, prev):
            if prev is None:
                return
            k, pc, pv = prev
            if k in "KQ":
                pe.wait_ge(s["kq_evac"], at(pv, KQ_N, pc + 1 + (NC if k == "Q" else 0)))
            elif k == "V":
                pe.wait_ge(s["v_done"], at(pv, NC, pc + 1))
            else:
                pe.wait_ge(s["m_evac"], at(pv, NC, pc + 1))

        class Pe:

            def __init__(self, pe):
                self.pe = pe

            def project(self, v, kind, c, prev):
                pe, b = self.pe, v[1]
                proj_free(pe, v, kind, c, prev)
                cols = slice(b * S + c * CH, b * S + (c + 1) * CH)
                if kind == "K":
                    if c == 0:
                        pe.wait_ge(s["w_in"], at((v[0], 0), W_DMA_N, 6 * 16))
                    nc.tensor.matmul(proj_ps[:], w_qkv[:, 1, :], xnT[:, cols],
                                     start=True, stop=True).then_inc(s["k_ps"], 1)
                elif kind == "Q":
                    nc.tensor.matmul(proj_ps[:], w_qkv[:, 0, :], xnT[:, cols],
                                     start=True, stop=True).then_inc(s["q_ps"], 1)
                elif kind == "V":
                    for t in range(TC):
                        at0 = b * S + c * CH + t * P
                        last = nc.tensor.matmul(proj_ps[:, t * P:(t + 1) * P], xnT[:, at0:at0 + P],
                                                w_qkv[:, 2, :], start=True, stop=True)
                    last.then_inc(s["v_ps"], 1)
                else:
                    pe.wait_ge(s["neg_max_done"], at(v, NC, c + 1))
                    nc.tensor.matmul(proj_ps[0:2 * TC, 0:P], neg_max[:, c % 2, :], ident[:],
                                     start=True, stop=True).then_inc(s["m_ps"], 1)

            def max_pair(self, v, r):
                pe, b = self.pe, v[1]
                c, qt, kc = r // (TC * NC), r // NC % TC, r % NC
                if qt == 0 and kc == 0:
                    pe.wait_ge(s["kq_hi_done"], at(v, KQ_N, NC + c + 1))
                if r == 0:
                    for j in range(2):
                        pe.wait_ge(k_dma[j], at(v, KQ_DMA_N, KQ_DMA_N))
                for h in range(2):
                    n = 2 * r + h
                    if not (is_first(v) and n < 2):
                        pe.wait_ge(s["max_done"], at(v, MAXN, n - 1))
                    rows = slice(h * HD, (h + 1) * HD)
                    nc.tensor.matmul(max_ps[h][:], q_hi[rows, c % 2, qt * P:(qt + 1) * P],
                                     k_dup[b][rows, h, kc * CH:(kc + 1) * CH],
                                     start=True, stop=True).then_inc(s["max_ready"], 1)

            def scores(self, u, st):
                pe, b = self.pe, u[1]
                c, kt = st // T, st % T
                cols, keys = slice(c * CH, (c + 1) * CH), slice(kt * P, (kt + 1) * P)
                if kt == 0:
                    pe.wait_ge(q_dma[c % 2], at(u, KQ_DMA_N, 6 * 16 * (c // 2 + 1)))
                    pe.wait_ge(m_dma[c % 2], at(u, M_DMA_N, 2 * 16 * (c // 2 + 1)))
                if st == 0 and is_first(u):
                    pe.wait_ge(s["ones_row"], 2)
                for h in range(2):
                    n = 2 * st + h
                    if not (is_first(u) and n < 2):
                        pe.wait_ge(s["exp_done"], at(u, SCORE_N, n - 1))
                    nc.tensor.matmul(score_ps[h][:], k_dup[b][:, h, keys], q_split[:, h, cols],
                                     start=True, stop=False)
                    nc.tensor.matmul(score_ps[h][:], k_low[b][:, h, keys], q_max[:, h, cols],
                                     start=False, stop=True).then_inc(s["score_ready"], 1)

            def values(self, u, st):
                pe, b = self.pe, u[1]
                c, kt = st // T, st % T
                if kt == 0 and not (is_first(u) and c < 2):
                    pe.wait_ge(s["o_norm_done"], at(u, NC, c - 1))
                if st == 0:
                    pe.wait_ge(s["v_done"], at(u, NC, NC))
                for h in range(2):
                    pe.wait_ge(s["exp_done"], at(u, SCORE_N, 2 * st + h + 1))
                    last = nc.tensor.matmul(o_ps[c % 2][h * HD:(h + 1) * HD, :],
                                            v_sb[b][:, kt, h * HD:(h + 1) * HD],
                                            probs[:, st % PRING, h, :],
                                            start=(kt == 0), stop=(kt == T - 1))
                last.then_inc(s["pv_done"], 1)

            def denominators(self, u, c):
                pe = self.pe
                pe.wait_ge(s["sum_all_done"], at(u, NC, c + 1))
                if not (is_first(u) and c == 0):
                    pe.wait_ge(s["y_done"], at(u, NC, c))
                for h in range(2):
                    last = nc.tensor.matmul(tail_ps[h * HD:(h + 1) * HD, :], ones[:], sum_all[:, h, :],
                                            start=True, stop=True)
                last.then_inc(s["denom_ps_ready"], 1)

            def out_projection(self, u, c):
                pe = self.pe
                pe.wait_ge(s["o_norm_done"], at(u, NC, c + 1))
                if c == 0 and u[1] == 0:
                    pe.wait_ge(s["wo_in"], at(u, WO_DMA_N, 16))
                for t in range(TC):
                    last = nc.tensor.matmul(tail_ps[:, t * D:(t + 1) * D], o_norm[:, t * P:(t + 1) * P],
                                            w_o[:], start=True, stop=True)
                last.then_inc(s["wo_ps_ready"], 1)

            def prepare_alone(self, v):
                prev = None
                for _, kind, c in PREP:
                    if kind == "M":
                        continue
                    self.project(v, kind, c, prev)
                    prev = (kind, c, v)
                    if kind == "Q":
                        for r in range(TC * NC * c, TC * NC * (c + 1)):
                            self.max_pair(v, r)
                        if c < NC - 1:
                            self.project(v, "M", c, prev)
                            prev = ("M", c, v)

            def unit(self, u, before, last=False):
                v = following(u)
                prev = (PREP[-1][1], PREP[-1][2], u) if before is not None else ("Q", NC - 1, u)
                for st in range(STEPS):
                    c, kt = st // T, st % T
                    self.scores(u, st)
                    if st:
                        self.values(u, st - 1)
                    elif before is not None:
                        self.values(before, STEPS - 1)
                    done = (u, c - 1) if c else (before, NC - 1)
                    if done[0] is not None:
                        if kt == DENOM_AT:
                            self.denominators(*done)
                        if kt == WO_AT:
                            self.out_projection(*done)
                    if not last:
                        for at_step, kind, pc in PREP:
                            if at_step == st:
                                self.project(v, kind, pc, prev)
                                prev = (kind, pc, v)
                        for r in range(PAIRS_OF_MAX):
                            if max_step(r) == st:
                                self.max_pair(v, r)
                    if st == M_LATE:
                        self.project(u, "M", NC - 1, prev)
                        prev = ("M", NC - 1, u)

        SUM_AT, DENOM_AT, NORM_AT, WO_AT, Y_AT = 2, 3, 4, 7, 8

        def act_evac(act, v, kind, c):
            if kind in "KQ":
                n = c + (NC if kind == "Q" else 0)
                act.wait_ge(s["k_ps" if kind == "K" else "q_ps"], at(v, NC, c + 1))
                if not (is_first(v) and n < 2):
                    act.wait_ge(s["kq_split"], at(v, KQ_N, n - 1))
                j = 1 if kind == "K" else 0
                hi = k_hi if kind == "K" else q_hi
                if not (is_first(v) and c < 2):
                    dma = k_dma if kind == "K" else q_dma
                    act.wait_ge(dma[c % 2], at(v, KQ_DMA_N, 6 * 16 * (c // 2)))
                    if kind == "Q":
                        act.wait_ge(s["max_ready"], at(v, MAXN, 2 * TC * NC * (c - 1)))
                nc.scalar.activation(hi[:, c % 2, :], proj_ps[:], ACT.Identity,
                                     bias=b_qk[:, j:j + 1]).then_inc(s["kq_hi_done"], 1)
                nc.scalar.activation(kq_f32[:, n % 2, :], proj_ps[:], ACT.Identity,
                                     bias=b_qk[:, j:j + 1]).then_inc(s["kq_evac"], 1)
            elif kind == "M":
                act.wait_ge(s["m_ps"], at(v, NC, c + 1))
                if not (is_first(v) and c < 2):
                    act.wait_ge(m_dma[c % 2], at(v, M_DMA_N, 2 * 16 * (c // 2)))
                nc.scalar.activation(max_rows[:, c % 2, :], proj_ps[0:2 * TC, 0:P],
                                     ACT.Copy).then_inc(s["m_evac"], 1)

        def act_unit(act, u, before, last=False):
            v = following(u)
            for st in range(STEPS):
                for h in range(2):
                    act.wait_ge(s["score_ready"], at(u, SCORE_N, 2 * st + h + 1))
                    if h == 0 and not (is_first(u) and st < PRING):
                        act.wait_ge(s["pv_done"], at(u, PV_N, st - PRING + 1))
                        if st >= PRING or before is not None:
                            w, ws = (u, st - PRING) if st >= PRING else (before, st - PRING + STEPS)
                            wc, wk = ws // T, ws % T
                            if wk % 2 == 0:
                                act.wait_ge(s["sum_even_done"], at(w, SUM_N, wc * (T // 2 - 1) + max(wk // 2, 1)))
                            else:
                                act.wait_ge(s["sum_odd_done"], at(w, SUM_N, wc * (T // 2 - 1) + max(wk // 2, 1)))
                    nc.scalar.activation(probs[:, st % PRING, h, :], score_ps[h][:], ACT.Exp,
                                         scale=SCALE).then_inc(s["exp_done"], 1)
                if not last:
                    for at_step, kind, pc in PREP:
                        if at_step == st:
                            act_evac(act, v, kind, pc)
                if st == M_LATE:
                    act_evac(act, u, "M", NC - 1)

        def dve_max(dve, v, r):
            for h in range(2):
                c, qt, kc = r // (TC * NC), r // NC % TC, r % NC
                dve.wait_ge(s["max_ready"], at(v, MAXN, 2 * r + h + 1))
                if qt == 0 and kc == 0 and h == 0 and not (is_first(v) and c < 2):
                    dve.wait_ge(s["neg_max_done"], at(v, NC, c - 1))
                nc.vector.reduce_max(max_part[:, c % 2, h * TC + qt, kc:kc + 1], max_ps[h][:],
                                     AX.X).then_inc(s["max_done"], 1)

        def dve_neg_max(dve, v, c):
            dve.wait_ge(s["max_done"], at(v, MAXN, 2 * TC * NC * (c + 1)))
            if not (is_first(v) and c < 2):
                dve.wait_ge(s["m_ps"], at(v, NC, c - 1))
            nc.vector.tensor_reduce(neg_max[:, c % 2, :], max_part[:, c % 2, :, :], AX.X, ALU.max,
                                    negate=True).then_inc(s["neg_max_done"], 1)

        def dve_v(dve, v, c, before_v):
            b = v[1]
            dve.wait_ge(s["v_ps"], at(v, NC, c + 1))
            if c == 0 and before_v is not None:
                dve.wait_ge(s["pv_done"], at(before_v, PV_N, PV_N))
            nc.vector.tensor_tensor(v_sb[b][:, c * TC:(c + 1) * TC, :],
                                    proj_ps[:].rearrange("p (t n) -> p t n", t=TC),
                                    b_v[:].unsqueeze(1).to_broadcast([P, TC, P]), ALU.add).then_inc(s["v_done"], 1)

        def dve_tail(dve, u, c, kt):
            if kt == SUM_AT:
                dve.wait_ge(s["sum_even_done"], at(u, SUM_N, (c + 1) * (T // 2 - 1)))
                dve.wait_ge(s["sum_odd_done"], at(u, SUM_N, (c + 1) * (T // 2 - 1)))
                if not (is_first(u) and c == 0):
                    dve.wait_ge(s["denom_ps_ready"], at(u, NC, c))
                nc.vector.tensor_tensor(sum_all[:], sum_even[:], sum_odd[:], ALU.add).then_inc(s["sum_all_done"], 1)
            if kt == NORM_AT:
                dve.wait_ge(s["denom_ps_ready"], at(u, NC, c + 1))
                nc.vector.reciprocal(denom[:], tail_ps[:]).then_inc(s["denom_done"], 1)
                dve.wait_ge(s["denom_done"], at(u, NC, c + 1))
                dve.wait_ge(s["pv_done"], at(u, PV_N, (c + 1) * T))
                if not (is_first(u) and c == 0):
                    dve.wait_ge(s["wo_ps_ready"], at(u, NC, c))
                nc.vector.tensor_tensor(o_norm[:], o_ps[c % 2][:], denom[:], ALU.mult).then_inc(s["o_norm_done"], 1)
            if kt == Y_AT:
                b = u[1]
                dve.wait_ge(s["wo_ps_ready"], at(u, NC, c + 1))
                part = y_acc[:, b * T + c * TC:b * T + (c + 1) * TC, :]
                nc.vector.tensor_tensor(part, tail_ps[:].rearrange("p (t n) -> p t n", t=TC), part,
                                        ALU.add).then_inc(s["y_done"], 1)

        def dve_even(dve, u, st):
            c, kt = st // T, st % T
            n = c * (T // 2 - 1) + kt // 2
            dve.wait_ge(s["exp_done"], at(u, SCORE_N, 2 * st + 2))
            if kt == 2:
                if not (is_first(u) and c == 0):
                    dve.wait_ge(s["sum_all_done"], at(u, NC, c))
                a = probs[:, (st - 2) % PRING, :, :]
            else:
                dve.wait_ge(s["sum_even_done"], at(u, SUM_N, n - 1))
                a = sum_even[:]
            nc.vector.tensor_tensor(sum_even[:], a, probs[:, st % PRING, :, :], ALU.add).then_inc(s["sum_even_done"], 1)

        def dve_unit(dve, u, before, last=False):
            v = following(u)
            for st in range(STEPS):
                c, kt = st // T, st % T
                if not last:
                    for r in range(PAIRS_OF_MAX):
                        if max_step(r) == st:
                            dve_max(dve, v, r)
                    for at_step, kind, pc in PREP:
                        if kind == "V" and at_step == st:
                            dve_v(dve, v, pc, before)
                        if kind == "M" and at_step - 1 == st:
                            dve_neg_max(dve, v, pc)
                if st == M_LATE - 1:
                    dve_neg_max(dve, u, NC - 1)
                if kt in (SUM_AT, NORM_AT, Y_AT):
                    done = (u, c - 1) if c else (before, NC - 1)
                    if done[0] is not None:
                        dve_tail(dve, *done, kt)
                if (kt - 1) % 2 == 0 and kt - 1 >= 2:
                    dve_even(dve, u, st - 1)

        def pool_split(pool, v, kind, c):
            n = c + (NC if kind == "Q" else 0)
            hi, lo = (k_hi, k_lo) if kind == "K" else (q_hi, q_lo)
            pool.wait_ge(s["kq_evac"], at(v, KQ_N, n + 1))
            nc.gpsimd.tensor_tensor(lo[:, c % 2, :], kq_f32[:, n % 2, :], hi[:, c % 2, :].bitcast(F32),
                                    ALU.subtract).then_inc(s["kq_split"], 1)

        def pool_odd(pool, u, st):
            c, kt = st // T, st % T
            n = c * (T // 2 - 1) + kt // 2
            pool.wait_ge(s["exp_done"], at(u, SCORE_N, 2 * st + 2))
            if kt == 3:
                if not (is_first(u) and c == 0):
                    pool.wait_ge(s["sum_all_done"], at(u, NC, c))
                a = probs[:, (st - 2) % PRING, :, :]
            else:
                pool.wait_ge(s["sum_odd_done"], at(u, SUM_N, n - 1))
                a = sum_odd[:]
            nc.gpsimd.tensor_tensor(sum_odd[:], a, probs[:, st % PRING, :, :], ALU.add).then_inc(s["sum_odd_done"], 1)

        def pool_unit(pool, u, before, last=False):
            v = following(u)
            for st in range(STEPS):
                kt = st % T
                if not last:
                    for at_step, kind, pc in PREP:
                        if kind in "KQ" and at_step == st:
                            pool_split(pool, v, kind, pc)
                if kt % 2 == 1 and kt >= 3:
                    pool_odd(pool, u, st)

        def sp_weights(sp, i):
            for dst, src in ((w_qkv[:, 0, :], wq_v[i]), (w_qkv[:, 1, :], wk_v[i]), (w_qkv[:, 2, :], wv_v[i]),
                             (b_qk[:, 0:1], bq_v[i].unsqueeze(1)), (b_qk[:, 1:2], bk_v[i].unsqueeze(1)),
                             (b_v[:], bv_v[i].partition_broadcast(P))):
                sp.dma_start(dst, src).then_inc(s["w_in"], 16)

        def sp_k(sp, v, c, free_after=None):
            b = v[1]
            split, read = at(v, KQ_N, c + 1), free_after and at(free_after, SCORE_N, 0)
            sp.wait_ge(s["kq_split"], split)
            if free_after is not None:
                sp.wait_ge(s["score_ready"], read)
            cols, j = slice(c * CH, (c + 1) * CH), c % 2
            for h in range(2):
                rows = slice(h * HD, (h + 1) * HD)
                sp.dma_start(k_dup[b][0:HD, h, cols].bitcast(F32), k_hi[rows, j, :].bitcast(F32)).then_inc(k_dma[j], 16)
                sp.dma_start(k_dup[b][HD:P, h, cols].bitcast(F32), k_hi[rows, j, :].bitcast(F32)).then_inc(k_dma[j], 16)
                sp.dma_start(k_low[b][0:HD, h, cols].bitcast(F32), k_lo[rows, j, :].bitcast(F32)).then_inc(k_dma[j], 16)

        def sp_q(sp, v, c, u):
            split, read = at(v, KQ_N, NC + c + 1), u and at(u, SCORE_N, 2 * T * (c + 1))
            sp.wait_ge(s["kq_split"], split)
            if u is not None:
                sp.wait_ge(s["score_ready"], read)
            cols, j = slice(c * CH, (c + 1) * CH), c % 2
            for h in range(2):
                rows = slice(h * HD, (h + 1) * HD)
                sp.dma_start(q_split[0:HD, h, cols].bitcast(F32), q_hi[rows, j, :].bitcast(F32)).then_inc(q_dma[j], 16)
                sp.dma_start(q_split[HD:P, h, cols].bitcast(F32), q_lo[rows, j, :].bitcast(F32)).then_inc(q_dma[j], 16)
                sp.dma_start(q_max[0:HD, h, cols].bitcast(F32), q_hi[rows, j, :].bitcast(F32)).then_inc(q_dma[j], 16)

        def sp_m(sp, v, c):
            sp.wait_ge(s["m_evac"], at(v, NC, c + 1))
            for h in range(2):
                dst = q_max[HD:HD + 1, h, c * CH:(c + 1) * CH].bitcast(F32).rearrange("o (t n) -> o t n", t=TC)
                sp.dma_start(dst, max_rows[h * TC:(h + 1) * TC, c % 2, :].bitcast(F32)).then_inc(m_dma[c % 2], 16)

        def sp_unit(sp, u, before, last=False):
            v = following(u)
            if last:
                sp_m(sp, u, NC - 1)
                return
            sp_k(sp, v, 0, free_after=None if before is None else u)
            sp_k(sp, v, 1)
            sp_m(sp, u, NC - 1)
            sp_k(sp, v, 2)
            sp_k(sp, v, 3)
            if u[1] == 0 and before is not None:
                sp.wait_ge(s["wo_ps_ready"], at(u, NC, 0))
                sp.dma_start(w_o[:], wo_v[number(u[0])]).then_inc(s["wo_in"], 16)
            for c in range(NC):
                if c == NC - 1 and u[1] == 0:
                    projected, evacuated, v_done = at(v, NC, NC), at(v, KQ_N, KQ_N), at(v, NC, NC)
                    sp.wait_ge(s["q_ps"], projected)
                    sp.wait_ge(s["kq_evac"], evacuated)
                    sp.wait_ge(s["v_done"], v_done)
                    if not isinstance(u[0], int) or u[0] < PAIRS - 1:
                        sp_weights(sp, number(u[0]) + 1)
                sp_q(sp, v, c, u)
                if c < NC - 1:
                    sp_m(sp, v, c)

        def units(name, eng, unit_fn):
            unit_fn(eng, (0, 0), None)
            unit_fn(eng, (0, 1), (0, 0))
            base = {n: eng.alloc_register(f"{name}_after_{n}") for n in UNIT_COUNTS}
            spare = [eng.alloc_register(f"{name}_wait_value{k}") for k in range(4)]
            for n, r in base.items():
                eng.reg_mov(r, B * n)
            with eng.Fori(1, PAIRS - 1) as number:
                i = Pair(eng, number, base, spare)
                unit_fn(eng, (i, 0), (i - 1, 1))
                unit_fn(eng, (i, 1), (i, 0))
                for n, r in base.items():
                    eng.reg_add(r, r, B * n)
            n = PAIRS - 1
            unit_fn(eng, (n, 0), (n - 1, 1))
            unit_fn(eng, (n, 1), (n, 0), last=True)

        NG = B * NC
        end = at((PAIRS - 1, B - 1), NC, NC)
        xg = sb("xg", [P, 2, TC, D])
        xn = probs[:].rearrange("p r h n -> p r (h n)")[:, :, 0:CH].rearrange("p r (t d) -> p r t d", t=TC)

        f_names = """f_ep1 f_ep2 f_ep3 ffn_w_in g_in0 g_in1 f_st1 f_mv1 f_rs1 f_yn f_x1 f_st2 f_mv2 f_rs2 f_xn f_xT_ps f_xT f_p_ps f_p
            f_h_ps f_h f_q_ps f_q f_z_ps f_z f_st3 f_mv3 f_rs3 f_zn f_out out_dma0 out_dma1""".split()
        f = {n: sem(n) for n in f_names}
        g_in = [f["g_in0"], f["g_in1"]]
        out_dma = [f["out_dma0"], f["out_dma1"]]
        v1 = probs[0:RANK, 2, 0, :]
        u1 = probs[:, 2, 1, 0:RANK]
        b1c = probs[:, 2, 1, RANK:RANK + FF // P]
        u2 = probs[:, 2, 1, P:2 * P].rearrange("p (f r) -> p f r", f=FF // P)
        v2 = probs[0:RANK, 3, 0, 0:D]
        b2r = probs[:, 3, 1, 0:D]
        hT = v_sb[0][:].rearrange("p t n -> p (t n)").rearrange("p (f n) -> p f n", f=FF // P)
        x1 = v_sb[1][:].rearrange("p t n -> p (t n)").rearrange("p (r t d) -> p r t d", r=4, t=TC)
        xnT2 = [sum_even[:, j, :] for j in range(2)]
        pT = [sum_odd[0:RANK, j, :] for j in range(2)]
        qT = [sum_all[0:RANK, j, :] for j in range(2)]
        z = [kq_f32[:, j, :].rearrange("p (t d) -> p t d", t=TC) for j in range(2)]

        block = ctx.enter_context(nc.Block())

        @block.sync
        def _(sp):
            for g in range(NG):
                if g >= 2:
                    sp.wait_ge(s["xn_done"], TC * (g - 1))
                sp.dma_start(xg[:, g % 2], x_v[:, g * TC:(g + 1) * TC, :]).then_inc(s[f"x_in{g % 2}"], 16)
                if g == 1:
                    sp_weights(sp, 0)
                    sp.dma_start(w_o[:], wo_v[0]).then_inc(s["wo_in"], 16)
                    sp.dma_start(y_acc[:, 0, :], bo.partition_broadcast(P)).then_inc(s["y_init"], 16)
            first = (0, 0)
            for c in range(NC):
                sp_k(sp, first, c)
            for c in range(NC):
                sp_q(sp, first, c, None)
                if c < NC - 1:
                    sp_m(sp, first, c)
            units("sp", sp, sp_unit)
            u = (PAIRS - 1, B - 1)
            sp.wait_ge(s["pv_done"], at(u, PV_N, PV_N))
            sp.wait_ge(s["sum_all_done"], at(u, NC, NC))
            for dst, src in ((u1, U1), (v1, V1), (b1c, b1.rearrange("(f p) -> p f", p=P)),
                             (u2, U2.rearrange("(f p) r -> p f r", p=P)), (v2, V2),
                             (b2r, b2.partition_broadcast(P))):
                sp.dma_start(dst, src, allow_slow_non_contiguous=dst is b1c).then_inc(f["ffn_w_in"], 16)
            for g in range(NG + 1):
                if g < NG:
                    if g >= 2:
                        sp.wait_ge(f["f_x1"], g - 1)
                    sp.dma_start(xg[:, g % 2], x_v[:, g * TC:(g + 1) * TC, :]).then_inc(g_in[g % 2], 16)
                if g >= 1:
                    sp.wait_ge(f["f_out"], g)
                    sp.dma_start(out_v[:, (g - 1) * TC:g * TC, :], z[(g - 1) % 2]).then_inc(out_dma[(g - 1) % 2], 16)
            for j in range(2):
                sp.wait_ge(out_dma[j], 16 * (NG // 2))

        @block.gpsimd
        def _(pool):
            def inverse_deviation(slot, mv_ready, added, rstd_ready, n):
                pool.wait_ge(mv_ready, n + 1)
                nc.gpsimd.tensor_scalar(ln_var[:, slot, :], ln_mv[:, slot, :, 1], EPS, None, ALU.add).then_inc(added, 1)
                pool.wait_ge(added, n + 1)
                nc.gpsimd.tensor_tensor(ln_rstd[:, slot, :], ln_var[:, slot, :], minus_half[:],
                                        ALU.pow).then_inc(rstd_ready, 1)

            nc.gpsimd.memset(minus_half[:], -0.5).then_inc(s["half_ready"], 1)
            pool.wait_ge(s["half_ready"], 1)
            nc.gpsimd.memset(ident[:], 0.0).then_inc(s["const_ready"], 1)
            pool.wait_ge(s["const_ready"], 1)
            nc.gpsimd.affine_select(out=ident[:], in_=ident[:], compare_op=ALU.not_equal, fill=1.0, base=0,
                                    pattern=[[-1, P]], channel_multiplier=1).then_inc(s["const_ready"], 1)
            nc.gpsimd.memset(ones[:], 1.0).then_inc(s["const_ready"], 1)
            pool.wait_ge(s["const_ready"], 3)
            for b in range(B):
                if b:
                    pool.wait_ge(s["ones_row"], b)
                nc.gpsimd.memset(k_low[b][HD:HD + 1, :, :].bitcast(F32), 1.0).then_inc(s["ones_row"], 1)
            pool.wait_ge(s["ones_row"], B)
            for g in range(NG):
                inverse_deviation(g % 2, s["mv_done"], s["eps_added"], s["rstd_done"], g)
            for c in range(NC):
                pool_split(pool, (0, 0), "K", c)
            for c in range(NC):
                pool_split(pool, (0, 0), "Q", c)
            units("pool", pool, pool_unit)
            for g in range(NG + 1):
                if g < NG:
                    inverse_deviation(0, f["f_mv1"], f["f_ep1"], f["f_rs1"], g)
                    inverse_deviation(0, f["f_mv2"], f["f_ep2"], f["f_rs2"], g)
                if g >= 1:
                    inverse_deviation(1, f["f_mv3"], f["f_ep3"], f["f_rs3"], g - 1)

        @block.scalar
        def _(act):
            for g in range(NG):
                act.wait_ge(s["xnT_ps_ready"], g + 1)
                nc.scalar.activation(xnT[:, g * CH:(g + 1) * CH], o_ps[g % 2][:], ACT.Copy).then_inc(s["xnT_done"], 1)
            first = (0, 0)
            for _, kind, c in PREP:
                if kind in "KQ":
                    act_evac(act, first, kind, c)
                if kind == "Q" and c < NC - 1:
                    act_evac(act, first, "M", c)
            units("act", act, act_unit)
            for g in range(NG):
                j = g % 2
                act.wait_ge(f["f_xT_ps"], g + 1)
                if g >= 2:
                    act.wait_ge(f["f_p_ps"], g - 1)
                nc.scalar.activation(xnT2[j], score_ps[0][:], ACT.Copy).then_inc(f["f_xT"], 1)
                act.wait_ge(f["f_p_ps"], g + 1)
                if g >= 2:
                    act.wait_ge(f["f_h_ps"], (g - 1) * (FF // P))
                nc.scalar.activation(pT[j], score_ps[1][0:RANK, :], ACT.Copy).then_inc(f["f_p"], 1)
                if g == 0:
                    act.wait_ge(f["ffn_w_in"], 6 * 16)
                for k in range(FF // P):
                    act.wait_ge(f["f_h_ps"], g * (FF // P) + k + 1)
                    if g >= 1 and k == 0:
                        act.wait_ge(f["f_q_ps"], g)
                    nc.scalar.activation(hT[:, k, :], (max_ps + o_ps)[k][:], ACT.Gelu_apprx_tanh,
                                         bias=b1c[:, k:k + 1]).then_inc(f["f_h"], 1)
                act.wait_ge(f["f_q_ps"], g + 1)
                if g >= 2:
                    act.wait_ge(f["f_z_ps"], g - 1)
                nc.scalar.activation(qT[j], proj_ps[0:RANK, :], ACT.Copy).then_inc(f["f_q"], 1)

        @block.vector
        def _(dve):
            ln_count = {}

            def layer_norm(tiles, outs, slot, S1, S2, S3, SO, n):
                for t in range(TC):
                    ins = nc.vector.bn_stats(ln_stats[:, slot, t, :], tiles[t])
                ins.then_inc(S1, 1)
                dve.wait_ge(S1, n + 1)
                for t in range(TC):
                    ins = nc.vector.bn_aggr(ln_mv[:, slot, t, :], ln_stats[:, slot, t, :])
                ins.then_inc(S2, 1)
                dve.wait_ge(S2, n + 1)
                dve.wait_ge(S3, n + 1)
                for t in range(TC):
                    ins = nc.vector.tensor_scalar(outs[t], tiles[t], ln_mv[:, slot, t, 0:1],
                                                  ln_rstd[:, slot, t:t + 1], ALU.subtract, ALU.mult)
                    ins.then_inc(SO, 1)

            for g in range(NG):
                j = g % 2
                dve.wait_ge(s[f"x_in{j}"], 16 * (g // 2 + 1))
                if g >= 2:
                    dve.wait_ge(s["xnT_ps_ready"], g - 1)
                layer_norm([xg[:, j, t, :] for t in range(TC)], [xn[:, j, t, :] for t in range(TC)], j,
                           s["stats_done"], s["mv_done"], s["rstd_done"], s["xn_done"], g)
            dve.wait_ge(s["y_init"], 16)
            nc.vector.tensor_copy(y_acc[:, 1:B * T, :], y_acc[:, 0:1, :].to_broadcast([P, B * T - 1, D])).then_inc(s["y_init"], 16)
            first = (0, 0)
            for _, kind, c in PREP:
                if kind == "V":
                    dve_v(dve, first, c, None)
                if kind == "Q":
                    for r in range(TC * NC * c, TC * NC * (c + 1)):
                        dve_max(dve, first, r)
                    if c < NC - 1:
                        dve_neg_max(dve, first, c)
            units("dve", dve, dve_unit)
            u = (PAIRS - 1, B - 1)
            dve_tail(dve, u, NC - 1, SUM_AT)
            dve_tail(dve, u, NC - 1, NORM_AT)
            dve_tail(dve, u, NC - 1, Y_AT)
            dve.wait_ge(s["y_done"], end)
            for g in range(NG + 1):
                if g < NG:
                    j = g % 2
                    yt = y_acc[:, g * TC:(g + 1) * TC, :]
                    layer_norm([yt[:, t, :] for t in range(TC)], [yt[:, t, :] for t in range(TC)], 0,
                               f["f_st1"], f["f_mv1"], f["f_rs1"], f["f_yn"], g)
                    dve.wait_ge(f["f_yn"], TC * (g + 1))
                    dve.wait_ge(g_in[j], 16 * (g // 2 + 1))
                    nc.vector.tensor_tensor(x1[:, g % 4], yt, xg[:, j], ALU.add).then_inc(f["f_x1"], 1)
                    dve.wait_ge(f["f_x1"], g + 1)
                    if g >= 2:
                        dve.wait_ge(f["f_xT_ps"], g - 1)
                    layer_norm([x1[:, g % 4, t, :] for t in range(TC)], [xn[:, j, t, :] for t in range(TC)], 0,
                               f["f_st2"], f["f_mv2"], f["f_rs2"], f["f_xn"], g)
                if g >= 1:
                    e = g - 1
                    j = e % 2
                    dve.wait_ge(f["f_z_ps"], e + 1)
                    if e == 0:
                        dve.wait_ge(f["ffn_w_in"], 6 * 16)
                    if e >= 2:
                        dve.wait_ge(out_dma[j], 16 * (e // 2))
                    nc.vector.tensor_tensor(z[j], tail_ps[:].rearrange("p (t d) -> p t d", t=TC),
                                            b2r.unsqueeze(1).to_broadcast([P, TC, D]), ALU.add).then_inc(f["f_z"], 1)
                    dve.wait_ge(f["f_z"], e + 1)
                    layer_norm([z[j][:, t, :] for t in range(TC)], [z[j][:, t, :] for t in range(TC)], 1,
                               f["f_st3"], f["f_mv3"], f["f_rs3"], f["f_zn"], e)
                    dve.wait_ge(f["f_zn"], TC * (e + 1))
                    nc.vector.tensor_tensor(z[j], z[j], x1[:, e % 4], ALU.add).then_inc(f["f_out"], 1)

        @block.tensor
        def _(pe):
            pe.wait_ge(s["const_ready"], 3)
            for g in range(NG):
                pe.wait_ge(s["xn_done"], TC * (g + 1))
                if g >= 2:
                    pe.wait_ge(s["xnT_done"], g - 1)
                for t in range(TC):
                    last = nc.tensor.transpose(o_ps[g % 2][:, t * P:(t + 1) * P], xn[:, g % 2, t, :], ident[:])
                last.then_inc(s["xnT_ps_ready"], 1)
            pe.wait_ge(s["xnT_done"], NG)
            me = Pe(pe)
            me.prepare_alone((0, 0))
            units("pe", pe, lambda _, u, before, last=False: me.unit(u, before, last))
            u = (PAIRS - 1, B - 1)
            me.values(u, STEPS - 1)
            me.denominators(u, NC - 1)
            me.out_projection(u, NC - 1)
            pe.wait_ge(f["ffn_w_in"], 6 * 16)
            for g in range(NG):
                j = g % 2
                pe.wait_ge(f["f_xn"], TC * (g + 1))
                if g >= 1:
                    pe.wait_ge(f["f_xT"], g)
                for t in range(TC):
                    last = nc.tensor.transpose(score_ps[0][:, t * P:(t + 1) * P], xn[:, j, t, :], ident[:])
                last.then_inc(f["f_xT_ps"], 1)
                pe.wait_ge(f["f_xT"], g + 1)
                if g >= 1:
                    pe.wait_ge(f["f_p"], g)
                nc.tensor.matmul(score_ps[1][0:RANK, :], u1, xnT2[j], start=True, stop=True).then_inc(f["f_p_ps"], 1)
                pe.wait_ge(f["f_p"], g + 1)
                for k in range(FF // P):
                    if g >= 1:
                        pe.wait_ge(f["f_h"], (g - 1) * (FF // P) + k + 1)
                    nc.tensor.matmul((max_ps + o_ps)[k][:], v1[:, k * P:(k + 1) * P], pT[j],
                                     start=True, stop=True).then_inc(f["f_h_ps"], 1)
                if g >= 1:
                    pe.wait_ge(f["f_q"], g)
                for k in range(FF // P):
                    pe.wait_ge(f["f_h"], g * (FF // P) + k + 1)
                    last = nc.tensor.matmul(proj_ps[0:RANK, :], u2[:, k, :], hT[:, k, :],
                                            start=(k == 0), stop=(k == FF // P - 1))
                last.then_inc(f["f_q_ps"], 1)
                pe.wait_ge(f["f_q"], g + 1)
                if g >= 1:
                    pe.wait_ge(f["f_z"], g)
                else:
                    pe.wait_ge(s["y_done"], end)
                for t in range(TC):
                    last = nc.tensor.matmul(tail_ps[:, t * D:(t + 1) * D], qT[j][:, t * P:(t + 1) * P], v2,
                                            start=True, stop=True)
                last.then_inc(f["f_z_ps"], 1)


_INS = ['L0_attn_x', 'L0_attn_Wq', 'L0_attn_bq', 'L0_attn_Wk', 'L0_attn_bk', 'L0_attn_Wv', 'L0_attn_bv',
        'L0_attn_Wo', 'L0_attn_bo', 'L0_ffn_U1', 'L0_ffn_V1', 'L0_ffn_b1', 'L0_ffn_U2', 'L0_ffn_V2', 'L0_ffn_b2']


def kernel(**inputs):
    import numpy as _np
    import concourse.bacc as _bacc
    from concourse import mybir as _mybir
    from concourse.bass_utils import run_bass_kernel_spmd as _run

    nc = _bacc.Bacc("TRN2", target_bir_lowering=False, num_devices=1)
    arrays, args = {}, []
    for name in _INS:
        a = _np.ascontiguousarray(inputs[name])
        arrays[f"in_{name}"] = a
        args.append(nc.dram_tensor(f"in_{name}", a.shape, _mybir.dt.from_np(a.dtype), kind="ExternalInput").ap())
    x = arrays["in_L0_attn_x"]
    args.append(nc.dram_tensor("block_out", x.shape, _mybir.dt.from_np(x.dtype), kind="ExternalOutput").ap())
    build(nc, *args)
    return _run(nc, [arrays], core_ids=[0]).results[0]["block_out"]
```

```python
import concourse.bass as bass
from concourse import mybir
from contextlib import ExitStack

F32 = mybir.dt.float32
F32R = mybir.dt.float32r
ALU = mybir.AluOpType
ACT = mybir.ActivationFunctionType
AX = mybir.AxisListType

P = 128
B, S, D = 2, 2048, 128
H, HD = 16, 64
FF, RANK = 512, 32
EPS = 1e-5
PAIRS = H // 2
T = S // P
CH = 512
NC = S // CH
TC = CH // P
STEPS = NC * T
PRING = 4
SCALE = float(HD) ** -0.5

SCORE_N = 2 * STEPS
PV_N = STEPS
MAXN = 2 * TC * NC * NC
DVE_TILES = [0, 2, 5, 8, 11, 15]
POOL_TILES = [t for t in range(T) if t not in DVE_TILES]
DVE_ADDS, POOL_ADDS = len(DVE_TILES) - 1, len(POOL_TILES) - 1
DVE_SUM_N, POOL_SUM_N = NC * DVE_ADDS, NC * POOL_ADDS
TAIL_DMA_N = NC * 2 * 16
KQ_N = 2 * NC
KQ_DMA_N = 6 * 16 * NC // 2
M_DMA_N = 2 * 16 * NC // 2

W_DMA_N = 6 * 16 // B
WO_DMA_N = 16 // B
UNIT_COUNTS = sorted({SCORE_N, PV_N, MAXN, DVE_SUM_N, POOL_SUM_N, TAIL_DMA_N, NC * 16, KQ_N, KQ_DMA_N, M_DMA_N, NC, W_DMA_N, WO_DMA_N})

K_AT = [0, 1, 5, 6]
V_AT = [3, 4, 9, 10]
Q_AT = [8, 18, 30, 44]
PAIRS_OF_MAX = TC * NC * NC
MAX_FIRST = 11


def max_step(r):
    return MAX_FIRST + r * (STEPS - MAX_FIRST) // PAIRS_OF_MAX


M_LAG = 4
M_AT = [max_step(TC * NC * (c + 1) - 1) + M_LAG for c in range(NC)]
M_LATE = M_AT[-1] - STEPS


def prep_order():
    ops = [(K_AT[c], "K", c) for c in range(NC)] + [(V_AT[c], "V", c) for c in range(NC)]
    ops += [(Q_AT[c], "Q", c) for c in range(NC)] + [(M_AT[c], "M", c) for c in range(NC - 1)]
    return sorted(ops)


PREP = prep_order()

SUM_AT, DENOM_AT, RECIP_AT, NORM_AT, WO_AT, Y_AT = 2, 3, 9, 13, 14, 15
WORK_BANKS = 4


def step_uses(st):
    c, kt = st // T, st % T
    done = (c - 1, "this") if c else (NC - 1, "before")
    uses = []
    if kt == DENOM_AT:
        uses.append(("L", *done))
    if kt == WO_AT:
        uses.append(("Wo", *done))
    uses += [(kind, pc, "next") for at_step, kind, pc in PREP if at_step == st]
    if st == M_LATE:
        uses.append(("M", NC - 1, "this"))
    pairs = [r for r in range(PAIRS_OF_MAX) if max_step(r) == st]
    return [("max", 2 * r + h, "next") for r in pairs for h in range(2)] + uses


UNIT_USES = [use for st in range(STEPS) for use in step_uses(st)]
assert len(UNIT_USES) % WORK_BANKS == 0
BANK = {(kind, n): k % WORK_BANKS for k, (kind, n, _) in enumerate(UNIT_USES)}




def build(nc, x, Wq, bq, Wk, bk, Wv, bv, Wo, bo, U1, V1, b1, U2, V2, b2, out):
    x_v = x.rearrange("b (t p) d -> p (b t) d", p=P)
    out_v = out.rearrange("b (t p) d -> p (b t) d", p=P)
    wq_v = Wq.rearrange("d (i h) k -> i d (h k)", h=2)
    wk_v = Wk.rearrange("d (i h) k -> i d (h k)", h=2)
    wv_v = Wv.rearrange("d (i h) k -> i d (h k)", h=2)
    wo_v = Wo.rearrange("(i h) k m -> i (h k) m", h=2)
    bq_v = bq.rearrange("(i h) k -> i (h k)", h=2)
    bk_v = bk.rearrange("(i h) k -> i (h k)", h=2)
    bv_v = bv.rearrange("(i h) k -> i (h k)", h=2)

    ctx = ExitStack()
    with ctx:
        def sb(name, shape, dt=F32):
            return ctx.enter_context(nc.sbuf_tensor(name, shape, dt))

        def sem(name):
            return ctx.enter_context(nc.semaphore(name))

        ident = sb("ident", [P, P])
        ones = sb("ones", [P, HD])
        xnT = sb("xnT", [P, B * S])
        y_acc = sb("y_acc", [P, B * T, D])
        w_qkv = sb("w_qkv", [P, 3, P])
        b_qk = sb("b_qk", [P, 2])
        b_v = sb("b_v", [P, P])
        w_o = sb("w_o", [P, D])
        k_dup = [sb(f"k_dup{b}", [P, 2, S], F32R) for b in range(B)]
        k_low = [sb(f"k_low{b}", [HD + 1, 2, S], F32R) for b in range(B)]
        q_split = sb("q_split", [P, 2, S], F32R)
        q_max = sb("q_max", [HD + 1, 2, S], F32R)
        v_sb = [sb(f"v_sb{b}", [P, T, P]) for b in range(B)]
        kq_f32 = sb("kq_f32", [P, 2, CH])
        k_hi = sb("k_hi", [P, 2, CH], F32R)
        k_lo = sb("k_lo", [P, 2, CH], F32R)
        q_hi = sb("q_hi", [P, 2, CH], F32R)
        q_lo = sb("q_lo", [P, 2, CH], F32R)
        probs = sb("probs", [P, PRING, 2, CH])
        dve_sum = sb("dve_sum", [P, 2, CH])
        pool_sum = sb("pool_sum", [P, 2, CH])
        sum_all = sb("sum_all", [P, 2, CH])
        denom = sb("denom", [P, CH])
        denom_col = sb("denom_col", [P, CH // HD])
        o_norm = sb("o_norm", [P, CH])
        max_part = sb("max_part", [P, 2, 2 * TC, NC])
        neg_max = sb("neg_max", [P, 2, 2 * TC])
        max_rows = sb("max_rows", [2 * TC, 2, P], F32R)
        ln_stats = sb("ln_stats", [P, 2, TC, 6])
        ln_mv = sb("ln_mv", [P, 2, TC, 2])
        ln_rstd = sb("ln_rstd", [P, 2, TC])
        ln_var = sb("ln_var", [P, 2, TC])
        minus_half = sb("minus_half", [P, TC])

        denom_dram = nc.dram_tensor("denom_scratch", (2, CH), F32, kind="Internal").ap()

        def bank(name):
            return ctx.enter_context(nc.psum_tensor(name, [P, CH], F32))

        score_ps = [bank(f"score_ps{h}") for h in range(2)]
        work = [bank(f"work{n}") for n in range(WORK_BANKS)]
        o_ps = [bank(f"o_ps{n}") for n in range(2)]

        names = """half_ready eps_added const_ready x_in0 x_in1 stats_done mv_done rstd_done xn_done xnT_ps_ready xnT_done y_init
            w_in wo_in k_ps q_ps v_ps m_ps kq_evac kq_hi_done kq_split v_done
            m_evac k_dma0 k_dma1 q_dma0 q_dma1 m_dma0 m_dma1 ones_row
            score_ready exp_done pv_done dve_sum_done pool_sum_done recip_done denom_copied col_dma scratch_dma denom_dma sum_all_done
            denom_ps_ready denom_done o_norm_done wo_ps_ready y_done max_ready max_done neg_max_done""".split()
        s = {n: sem(n) for n in names}
        k_dma, q_dma, m_dma = ([s[f"{n}_dma{j}"] for j in range(2)] for n in "kqm")

        class Pair:

            def __init__(self, eng, number, base, spare, shift=0):
                self.eng, self.number, self.base, self.spare, self.shift = eng, number, base, spare, shift

            def __add__(self, n):
                return Pair(self.eng, self.number, self.base, self.spare, self.shift + n)

            def __sub__(self, n):
                return self + -n

        def at(unit, per_unit, n):
            i, b = unit
            n += b * per_unit
            if isinstance(i, int):
                return i * B * per_unit + n
            n += i.shift * B * per_unit
            if n == 0:
                return i.base[per_unit]
            spare = i.spare.pop(0)
            i.spare.append(spare)
            i.eng.reg_add(spare, i.base[per_unit], n)
            return spare

        def number(i):
            return i if isinstance(i, int) else i.number + i.shift

        def is_first(unit):
            return isinstance(unit[0], int) and unit == (0, 0)

        def following(unit):
            i, b = unit
            return (i, 1) if b == 0 else (i + 1, 0)


        class Pe:

            def __init__(self, pe):
                self.pe = pe
                self.user = {}

            def take(self, kind, n, unit):
                bank = BANK[kind, n]
                if bank in self.user:
                    was, k, w = self.user[bank]
                    if was == "max":
                        self.pe.wait_ge(s["max_done"], at(w, MAXN, k + 1))
                    elif was in "KQ":
                        self.pe.wait_ge(s["kq_evac"], at(w, KQ_N, k + 1 + (NC if was == "Q" else 0)))
                    elif was == "V":
                        self.pe.wait_ge(s["v_done"], at(w, NC, k + 1))
                    elif was == "M":
                        self.pe.wait_ge(s["m_evac"], at(w, NC, k + 1))
                    elif was == "L":
                        self.pe.wait_ge(s["denom_copied"], at(w, NC, k + 1))
                    else:
                        self.pe.wait_ge(s["y_done"], at(w, NC, k + 1))
                self.user[bank] = (kind, n, unit)
                return work[bank]

            def project(self, v, kind, c):
                pe, b = self.pe, v[1]
                proj_ps = self.take(kind, c, v)
                cols = slice(b * S + c * CH, b * S + (c + 1) * CH)
                if kind == "K":
                    if c == 0:
                        pe.wait_ge(s["w_in"], at((v[0], 0), W_DMA_N, 6 * 16))
                    nc.tensor.matmul(proj_ps[:], w_qkv[:, 1, :], xnT[:, cols],
                                     start=True, stop=True).then_inc(s["k_ps"], 1)
                elif kind == "Q":
                    nc.tensor.matmul(proj_ps[:], w_qkv[:, 0, :], xnT[:, cols],
                                     start=True, stop=True).then_inc(s["q_ps"], 1)
                elif kind == "V":
                    for t in range(TC):
                        at0 = b * S + c * CH + t * P
                        last = nc.tensor.matmul(proj_ps[:, t * P:(t + 1) * P], xnT[:, at0:at0 + P],
                                                w_qkv[:, 2, :], start=True, stop=True)
                    last.then_inc(s["v_ps"], 1)
                else:
                    pe.wait_ge(s["neg_max_done"], at(v, NC, c + 1))
                    nc.tensor.matmul(proj_ps[0:2 * TC, 0:P], neg_max[:, c % 2, :], ident[:],
                                     start=True, stop=True).then_inc(s["m_ps"], 1)

            def max_pair(self, v, r):
                pe, b = self.pe, v[1]
                c, qt, kc = r // (TC * NC), r // NC % TC, r % NC
                if qt == 0 and kc == 0:
                    pe.wait_ge(s["kq_hi_done"], at(v, KQ_N, NC + c + 1))
                if r == 0:
                    for j in range(2):
                        pe.wait_ge(k_dma[j], at(v, KQ_DMA_N, KQ_DMA_N))
                for h in range(2):
                    max_ps = self.take("max", 2 * r + h, v)
                    rows = slice(h * HD, (h + 1) * HD)
                    nc.tensor.matmul(max_ps[:], q_hi[rows, c % 2, qt * P:(qt + 1) * P],
                                     k_dup[b][rows, h, kc * CH:(kc + 1) * CH],
                                     start=True, stop=True).then_inc(s["max_ready"], 1)

            def scores(self, u, st):
                pe, b = self.pe, u[1]
                c, kt = st // T, st % T
                cols, keys = slice(c * CH, (c + 1) * CH), slice(kt * P, (kt + 1) * P)
                if kt == 0:
                    pe.wait_ge(q_dma[c % 2], at(u, KQ_DMA_N, 6 * 16 * (c // 2 + 1)))
                    pe.wait_ge(m_dma[c % 2], at(u, M_DMA_N, 2 * 16 * (c // 2 + 1)))
                if st == 0 and is_first(u):
                    pe.wait_ge(s["ones_row"], 2)
                for h in range(2):
                    n = 2 * st + h
                    if not (is_first(u) and n < 2):
                        pe.wait_ge(s["exp_done"], at(u, SCORE_N, n - 1))
                    nc.tensor.matmul(score_ps[h][:], k_dup[b][:, h, keys], q_split[:, h, cols],
                                     start=True, stop=False)
                    nc.tensor.matmul(score_ps[h][:], k_low[b][:, h, keys], q_max[:, h, cols],
                                     start=False, stop=True).then_inc(s["score_ready"], 1)

            def values(self, u, st):
                pe, b = self.pe, u[1]
                c, kt = st // T, st % T
                if kt == 0 and not (is_first(u) and c < 2):
                    pe.wait_ge(s["o_norm_done"], at(u, NC, c - 1))
                if st == 0:
                    pe.wait_ge(s["v_done"], at(u, NC, NC))
                for h in range(2):
                    pe.wait_ge(s["exp_done"], at(u, SCORE_N, 2 * st + h + 1))
                    last = nc.tensor.matmul(o_ps[c % 2][h * HD:(h + 1) * HD, :],
                                            v_sb[b][:, kt, h * HD:(h + 1) * HD],
                                            probs[:, st % PRING, h, :],
                                            start=(kt == 0), stop=(kt == T - 1))
                last.then_inc(s["pv_done"], 1)

            def denominators(self, u, c):
                pe = self.pe
                pe.wait_ge(s["sum_all_done"], at(u, NC, c + 1))
                tail_ps = self.take("L", c, u)
                for h in range(2):
                    last = nc.tensor.matmul(tail_ps[h * HD:(h + 1) * HD, :], ones[:], sum_all[:, h, :],
                                            start=True, stop=True)
                last.then_inc(s["denom_ps_ready"], 1)

            def out_projection(self, u, c):
                pe = self.pe
                pe.wait_ge(s["o_norm_done"], at(u, NC, c + 1))
                if c == 0 and u[1] == 0:
                    pe.wait_ge(s["wo_in"], at(u, WO_DMA_N, 16))
                tail_ps = self.take("Wo", c, u)
                for t in range(TC):
                    last = nc.tensor.matmul(tail_ps[:, t * D:(t + 1) * D], o_norm[:, t * P:(t + 1) * P],
                                            w_o[:], start=True, stop=True)
                last.then_inc(s["wo_ps_ready"], 1)

            def prepare_alone(self, v):
                for _, kind, c in PREP:
                    if kind == "M":
                        continue
                    self.project(v, kind, c)
                    if kind == "Q":
                        for r in range(TC * NC * c, TC * NC * (c + 1)):
                            self.max_pair(v, r)
                        if c < NC - 1:
                            self.project(v, "M", c)

            def unit(self, u, before, last=False):
                whose = {"before": before, "this": u, "next": None if last else following(u)}
                if before is not None:
                    ended = {"this": before, "next": u}
                    for kind, n, who in UNIT_USES[-WORK_BANKS:]:
                        self.user[BANK[kind, n]] = (kind, n, ended[who])
                for st in range(STEPS):
                    self.scores(u, st)
                    uses = [(kind, n, whose[who]) for kind, n, who in step_uses(st) if whose[who] is not None]
                    pairs = [n // 2 for kind, n, _ in uses if kind == "max" and n % 2 == 0]
                    for r in pairs[:1]:
                        self.max_pair(whose["next"], r)
                    if st:
                        self.values(u, st - 1)
                    elif before is not None:
                        self.values(before, STEPS - 1)
                    for r in pairs[1:]:
                        self.max_pair(whose["next"], r)
                    for kind, n, unit in uses:
                        if kind == "L":
                            self.denominators(unit, n)
                        elif kind == "Wo":
                            self.out_projection(unit, n)
                        elif kind != "max":
                            self.project(unit, kind, n)

        def act_evac(act, v, kind, c):
            proj_ps = work[BANK[kind, c]] if kind != "V" else None
            if kind in "KQ":
                n = c + (NC if kind == "Q" else 0)
                act.wait_ge(s["k_ps" if kind == "K" else "q_ps"], at(v, NC, c + 1))
                if not (is_first(v) and n < 2):
                    act.wait_ge(s["kq_split"], at(v, KQ_N, n - 1))
                j = 1 if kind == "K" else 0
                hi = k_hi if kind == "K" else q_hi
                if not (is_first(v) and c < 2):
                    dma = k_dma if kind == "K" else q_dma
                    act.wait_ge(dma[c % 2], at(v, KQ_DMA_N, 6 * 16 * (c // 2)))
                    if kind == "Q":
                        act.wait_ge(s["max_ready"], at(v, MAXN, 2 * TC * NC * (c - 1)))
                nc.scalar.activation(hi[:, c % 2, :], proj_ps[:], ACT.Identity,
                                     bias=b_qk[:, j:j + 1]).then_inc(s["kq_hi_done"], 1)
                nc.scalar.activation(kq_f32[:, n % 2, :], proj_ps[:], ACT.Identity,
                                     bias=b_qk[:, j:j + 1]).then_inc(s["kq_evac"], 1)
            elif kind == "M":
                act.wait_ge(s["m_ps"], at(v, NC, c + 1))
                if not (is_first(v) and c < 2):
                    act.wait_ge(m_dma[c % 2], at(v, M_DMA_N, 2 * 16 * (c // 2)))
                nc.scalar.activation(max_rows[:, c % 2, :], proj_ps[0:2 * TC, 0:P],
                                     ACT.Copy).then_inc(s["m_evac"], 1)

        def act_denom(act, u, c):
            act.wait_ge(s["denom_ps_ready"], at(u, NC, c + 1))
            if not (is_first(u) and c == 0):
                act.wait_ge(s["o_norm_done"], at(u, NC, c))
            nc.scalar.activation(denom[:], work[BANK["L", c]][:], ACT.Copy).then_inc(s["denom_copied"], 1)

        def act_unit(act, u, before, last=False):
            v = following(u)
            for st in range(STEPS):
                for h in range(2):
                    act.wait_ge(s["score_ready"], at(u, SCORE_N, 2 * st + h + 1))
                    if h == 0 and not (is_first(u) and st < PRING):
                        act.wait_ge(s["pv_done"], at(u, PV_N, st - PRING + 1))
                        if st >= PRING or before is not None:
                            w, ws = (u, st - PRING) if st >= PRING else (before, st - PRING + STEPS)
                            wc, wk = ws // T, ws % T
                            if wk in DVE_TILES:
                                act.wait_ge(s["dve_sum_done"], at(w, DVE_SUM_N, wc * DVE_ADDS + max(DVE_TILES.index(wk), 1)))
                            else:
                                act.wait_ge(s["pool_sum_done"], at(w, POOL_SUM_N, wc * POOL_ADDS + max(POOL_TILES.index(wk), 1)))
                    nc.scalar.activation(probs[:, st % PRING, h, :], score_ps[h][:], ACT.Exp,
                                         scale=SCALE).then_inc(s["exp_done"], 1)
                done = (u, st // T - 1) if st >= T else (before, NC - 1)
                if done[0] is not None and st % T == DENOM_AT:
                    act_denom(act, *done)
                if not last:
                    for at_step, kind, pc in PREP:
                        if at_step == st:
                            act_evac(act, v, kind, pc)
                if st == M_LATE:
                    act_evac(act, u, "M", NC - 1)

        def dve_max(dve, v, r):
            for h in range(2):
                c, qt, kc = r // (TC * NC), r // NC % TC, r % NC
                dve.wait_ge(s["max_ready"], at(v, MAXN, 2 * r + h + 1))
                if qt == 0 and kc == 0 and h == 0 and not (is_first(v) and c < 2):
                    dve.wait_ge(s["neg_max_done"], at(v, NC, c - 1))
                nc.vector.reduce_max(max_part[:, c % 2, h * TC + qt, kc:kc + 1], work[BANK["max", 2 * r + h]][:],
                                     AX.X).then_inc(s["max_done"], 1)

        def dve_neg_max(dve, v, c):
            dve.wait_ge(s["max_done"], at(v, MAXN, 2 * TC * NC * (c + 1)))
            if not (is_first(v) and c < 2):
                dve.wait_ge(s["m_ps"], at(v, NC, c - 1))
            nc.vector.tensor_reduce(neg_max[:, c % 2, :], max_part[:, c % 2, :, :], AX.X, ALU.max,
                                    negate=True).then_inc(s["neg_max_done"], 1)

        def dve_v(dve, v, c, before_v):
            b = v[1]
            dve.wait_ge(s["v_ps"], at(v, NC, c + 1))
            if c == 0 and before_v is not None:
                dve.wait_ge(s["pv_done"], at(before_v, PV_N, PV_N))
            nc.vector.tensor_tensor(v_sb[b][:, c * TC:(c + 1) * TC, :],
                                    work[BANK["V", c]][:].rearrange("p (t n) -> p t n", t=TC),
                                    b_v[:].unsqueeze(1).to_broadcast([P, TC, P]), ALU.add).then_inc(s["v_done"], 1)

        def dve_tail(dve, u, c, kt):
            if kt == SUM_AT:
                dve.wait_ge(s["dve_sum_done"], at(u, DVE_SUM_N, (c + 1) * DVE_ADDS))
                dve.wait_ge(s["pool_sum_done"], at(u, POOL_SUM_N, (c + 1) * POOL_ADDS))
                if not (is_first(u) and c == 0):
                    dve.wait_ge(s["denom_ps_ready"], at(u, NC, c))
                nc.vector.tensor_tensor(sum_all[:], dve_sum[:], pool_sum[:], ALU.add).then_inc(s["sum_all_done"], 1)
            if kt == RECIP_AT:
                dve.wait_ge(s["col_dma"], at(u, TAIL_DMA_N, 2 * 16 * (c + 1)))
                nc.vector.reciprocal(denom_col[:], denom_col[:]).then_inc(s["recip_done"], 1)
            if kt == NORM_AT:
                dve.wait_ge(s["denom_dma"], at(u, TAIL_DMA_N, 2 * 16 * (c + 1)))
                dve.wait_ge(s["pv_done"], at(u, PV_N, (c + 1) * T))
                if not (is_first(u) and c == 0):
                    dve.wait_ge(s["wo_ps_ready"], at(u, NC, c))
                nc.vector.tensor_tensor(o_norm[:], o_ps[c % 2][:], denom[:], ALU.mult).then_inc(s["o_norm_done"], 1)
            if kt == Y_AT:
                b = u[1]
                dve.wait_ge(s["wo_ps_ready"], at(u, NC, c + 1))
                part = y_acc[:, b * T + c * TC:b * T + (c + 1) * TC, :]
                nc.vector.tensor_tensor(part, work[BANK["Wo", c]][:].rearrange("p (t n) -> p t n", t=TC), part,
                                        ALU.add).then_inc(s["y_done"], 1)

        def add_tile(eng, u, st, tiles, done, total):
            c, kt = st // T, st % T
            k, adds = tiles.index(kt), len(tiles) - 1
            if k == 0:
                return
            eng.wait_ge(s["exp_done"], at(u, SCORE_N, 2 * st + 2))
            if k == 1:
                if not (is_first(u) and c == 0):
                    eng.wait_ge(s["sum_all_done"], at(u, NC, c))
                so_far = probs[:, (st - kt + tiles[0]) % PRING, :, :]
            else:
                eng.wait_ge(done, at(u, NC * adds, c * adds + k - 1))
                so_far = total[:]
            eng.tensor_tensor(total[:], so_far, probs[:, st % PRING, :, :], ALU.add).then_inc(done, 1)

        def dve_unit(dve, u, before, last=False):
            v = following(u)
            for st in range(STEPS):
                c, kt = st // T, st % T
                done = (u, c - 1) if c else (before, NC - 1)
                if kt == Y_AT and done[0] is not None:
                    dve_tail(dve, *done, kt)
                if not last:
                    for r in range(PAIRS_OF_MAX):
                        if max_step(r) == st:
                            dve_max(dve, v, r)
                    for at_step, kind, pc in PREP:
                        if kind == "V" and at_step == st:
                            dve_v(dve, v, pc, before)
                        if kind == "M" and at_step - 1 == st:
                            dve_neg_max(dve, v, pc)
                if st == M_LATE - 1:
                    dve_neg_max(dve, u, NC - 1)
                if kt in (SUM_AT, RECIP_AT, NORM_AT) and done[0] is not None:
                    dve_tail(dve, *done, kt)
                if st and (st - 1) % T in DVE_TILES:
                    add_tile(dve, u, st - 1, DVE_TILES, s["dve_sum_done"], dve_sum)
                elif st == 0 and before is not None and T - 1 in DVE_TILES:
                    add_tile(dve, before, STEPS - 1, DVE_TILES, s["dve_sum_done"], dve_sum)

        def pool_split(pool, v, kind, c):
            n = c + (NC if kind == "Q" else 0)
            hi, lo = (k_hi, k_lo) if kind == "K" else (q_hi, q_lo)
            pool.wait_ge(s["kq_evac"], at(v, KQ_N, n + 1))
            nc.gpsimd.tensor_tensor(lo[:, c % 2, :], kq_f32[:, n % 2, :], hi[:, c % 2, :].bitcast(F32),
                                    ALU.subtract).then_inc(s["kq_split"], 1)

        def pool_unit(pool, u, before, last=False):
            v = following(u)
            for st in range(STEPS):
                kt = st % T
                if not last:
                    for at_step, kind, pc in PREP:
                        if kind in "KQ" and at_step == st:
                            pool_split(pool, v, kind, pc)
                if kt in POOL_TILES:
                    add_tile(pool, u, st, POOL_TILES, s["pool_sum_done"], pool_sum)

        def sp_weights(sp, i):
            for dst, src in ((w_qkv[:, 0, :], wq_v[i]), (w_qkv[:, 1, :], wk_v[i]), (w_qkv[:, 2, :], wv_v[i]),
                             (b_qk[:, 0:1], bq_v[i].unsqueeze(1)), (b_qk[:, 1:2], bk_v[i].unsqueeze(1)),
                             (b_v[:], bv_v[i].partition_broadcast(P))):
                sp.dma_start(dst, src).then_inc(s["w_in"], 16)

        def sp_k(sp, v, c, free_after=None):
            b = v[1]
            split, read = at(v, KQ_N, c + 1), free_after and at(free_after, SCORE_N, 0)
            sp.wait_ge(s["kq_split"], split)
            if free_after is not None:
                sp.wait_ge(s["score_ready"], read)
            cols, j = slice(c * CH, (c + 1) * CH), c % 2
            for h in range(2):
                rows = slice(h * HD, (h + 1) * HD)
                sp.dma_start(k_dup[b][0:HD, h, cols].bitcast(F32), k_hi[rows, j, :].bitcast(F32)).then_inc(k_dma[j], 16)
                sp.dma_start(k_dup[b][HD:P, h, cols].bitcast(F32), k_hi[rows, j, :].bitcast(F32)).then_inc(k_dma[j], 16)
                sp.dma_start(k_low[b][0:HD, h, cols].bitcast(F32), k_lo[rows, j, :].bitcast(F32)).then_inc(k_dma[j], 16)

        def sp_q(sp, v, c, u):
            split, read = at(v, KQ_N, NC + c + 1), u and at(u, SCORE_N, 2 * T * (c + 1))
            sp.wait_ge(s["kq_split"], split)
            if u is not None:
                sp.wait_ge(s["score_ready"], read)
            cols, j = slice(c * CH, (c + 1) * CH), c % 2
            for h in range(2):
                rows = slice(h * HD, (h + 1) * HD)
                sp.dma_start(q_split[0:HD, h, cols].bitcast(F32), q_hi[rows, j, :].bitcast(F32)).then_inc(q_dma[j], 16)
                sp.dma_start(q_split[HD:P, h, cols].bitcast(F32), q_lo[rows, j, :].bitcast(F32)).then_inc(q_dma[j], 16)
                sp.dma_start(q_max[0:HD, h, cols].bitcast(F32), q_hi[rows, j, :].bitcast(F32)).then_inc(q_dma[j], 16)

        def sp_denom(sp, u, c):
            sp.wait_ge(s["denom_copied"], at(u, NC, c + 1))
            for h in range(2):
                rows = slice(h * HD, (h + 1) * HD)
                sp.dma_start(denom_col[rows, :], denom[h * HD:h * HD + 1, :]).then_inc(s["col_dma"], 16)
            sp.wait_ge(s["recip_done"], at(u, NC, c + 1))
            sp.dma_start(denom_dram.rearrange("h (p n) -> (h p) n", p=HD), denom_col[:]).then_inc(s["scratch_dma"], 16)
            sp.wait_ge(s["scratch_dma"], at(u, NC * 16, 16 * (c + 1)))
            for h in range(2):
                sp.dma_start(denom[h * HD:(h + 1) * HD, :],
                             denom_dram[h].partition_broadcast(HD)).then_inc(s["denom_dma"], 16)

        def sp_m(sp, v, c):
            sp.wait_ge(s["m_evac"], at(v, NC, c + 1))
            for h in range(2):
                dst = q_max[HD:HD + 1, h, c * CH:(c + 1) * CH].bitcast(F32).rearrange("o (t n) -> o t n", t=TC)
                sp.dma_start(dst, max_rows[h * TC:(h + 1) * TC, c % 2, :].bitcast(F32)).then_inc(m_dma[c % 2], 16)

        def sp_unit(sp, u, before, last=False):
            v = following(u)
            if last:
                sp_m(sp, u, NC - 1)
                sp_denom(sp, before, NC - 1)
                for c in range(NC):
                    sp_denom(sp, u, c)
                return
            sp_k(sp, v, 0, free_after=None if before is None else u)
            sp_k(sp, v, 1)
            sp_m(sp, u, NC - 1)
            sp_k(sp, v, 2)
            sp_k(sp, v, 3)
            if before is not None:
                sp_denom(sp, before, NC - 1)
            if u[1] == 0 and before is not None:
                sp.wait_ge(s["wo_ps_ready"], at(u, NC, 0))
                sp.dma_start(w_o[:], wo_v[number(u[0])]).then_inc(s["wo_in"], 16)
            for c in range(NC):
                if c == NC - 1 and u[1] == 0:
                    projected, evacuated, v_done = at(v, NC, NC), at(v, KQ_N, KQ_N), at(v, NC, NC)
                    sp.wait_ge(s["q_ps"], projected)
                    sp.wait_ge(s["kq_evac"], evacuated)
                    sp.wait_ge(s["v_done"], v_done)
                    if not isinstance(u[0], int) or u[0] < PAIRS - 1:
                        sp_weights(sp, number(u[0]) + 1)
                sp_q(sp, v, c, u)
                if c < NC - 1:
                    sp_denom(sp, u, c)
                    sp_m(sp, v, c)

        def units(name, eng, unit_fn):
            unit_fn(eng, (0, 0), None)
            unit_fn(eng, (0, 1), (0, 0))
            base = {n: eng.alloc_register(f"{name}_after_{n}") for n in UNIT_COUNTS}
            spare = [eng.alloc_register(f"{name}_wait_value{k}") for k in range(4)]
            for n, r in base.items():
                eng.reg_mov(r, B * n)
            with eng.Fori(1, PAIRS - 1) as number:
                i = Pair(eng, number, base, spare)
                unit_fn(eng, (i, 0), (i - 1, 1))
                unit_fn(eng, (i, 1), (i, 0))
                for n, r in base.items():
                    eng.reg_add(r, r, B * n)
            n = PAIRS - 1
            unit_fn(eng, (n, 0), (n - 1, 1))
            unit_fn(eng, (n, 1), (n, 0), last=True)

        NG = B * NC
        end = at((PAIRS - 1, B - 1), NC, NC)
        xg = sb("xg", [P, 2, TC, D])
        xn = probs[:].rearrange("p r h n -> p r (h n)")[:, :, 0:CH].rearrange("p r (t d) -> p r t d", t=TC)

        f_names = """f_ep1 f_ep2 f_ep3 ffn_w_in g_in0 g_in1 f_st1 f_mv1 f_rs1 f_yn f_x1 f_st2 f_mv2 f_rs2 f_xn f_xT_ps f_xT f_p_ps f_p
            f_h_ps f_h f_q_ps f_q f_z_ps f_z f_st3 f_mv3 f_rs3 f_zn f_out out_dma0 out_dma1""".split()
        f = {n: sem(n) for n in f_names}
        g_in = [f["g_in0"], f["g_in1"]]
        out_dma = [f["out_dma0"], f["out_dma1"]]
        v1 = probs[0:RANK, 2, 0, :]
        u1 = probs[:, 2, 1, 0:RANK]
        b1c = probs[:, 2, 1, RANK:RANK + FF // P]
        u2 = probs[:, 2, 1, P:2 * P].rearrange("p (f r) -> p f r", f=FF // P)
        v2 = probs[0:RANK, 3, 0, 0:D]
        b2r = probs[:, 3, 1, 0:D]
        hT = v_sb[0][:].rearrange("p t n -> p (t n)").rearrange("p (f n) -> p f n", f=FF // P)
        x1 = v_sb[1][:].rearrange("p t n -> p (t n)").rearrange("p (r t d) -> p r t d", r=4, t=TC)
        xnT2 = [dve_sum[:, j, :] for j in range(2)]
        pT = [pool_sum[0:RANK, j, :] for j in range(2)]
        qT = [sum_all[0:RANK, j, :] for j in range(2)]
        z = [kq_f32[:, j, :].rearrange("p (t d) -> p t d", t=TC) for j in range(2)]

        block = ctx.enter_context(nc.Block())

        @block.sync
        def _(sp):
            for g in range(NG):
                if g >= 2:
                    sp.wait_ge(s["xn_done"], TC * (g - 1))
                sp.dma_start(xg[:, g % 2], x_v[:, g * TC:(g + 1) * TC, :]).then_inc(s[f"x_in{g % 2}"], 16)
                if g == 1:
                    sp_weights(sp, 0)
                    sp.dma_start(w_o[:], wo_v[0]).then_inc(s["wo_in"], 16)
                    sp.dma_start(y_acc[:, 0, :], bo.partition_broadcast(P)).then_inc(s["y_init"], 16)
            first = (0, 0)
            for c in range(NC):
                sp_k(sp, first, c)
            for c in range(NC):
                sp_q(sp, first, c, None)
                if c < NC - 1:
                    sp_m(sp, first, c)
            units("sp", sp, sp_unit)
            u = (PAIRS - 1, B - 1)
            sp.wait_ge(s["pv_done"], at(u, PV_N, PV_N))
            sp.wait_ge(s["sum_all_done"], at(u, NC, NC))
            for dst, src in ((u1, U1), (v1, V1), (b1c, b1.rearrange("(f p) -> p f", p=P)),
                             (u2, U2.rearrange("(f p) r -> p f r", p=P)), (v2, V2),
                             (b2r, b2.partition_broadcast(P))):
                sp.dma_start(dst, src, allow_slow_non_contiguous=dst is b1c).then_inc(f["ffn_w_in"], 16)
            for g in range(NG + 1):
                if g < NG:
                    if g >= 2:
                        sp.wait_ge(f["f_x1"], g - 1)
                    sp.dma_start(xg[:, g % 2], x_v[:, g * TC:(g + 1) * TC, :]).then_inc(g_in[g % 2], 16)
                if g >= 1:
                    sp.wait_ge(f["f_out"], g)
                    sp.dma_start(out_v[:, (g - 1) * TC:g * TC, :], z[(g - 1) % 2]).then_inc(out_dma[(g - 1) % 2], 16)
            for j in range(2):
                sp.wait_ge(out_dma[j], 16 * (NG // 2))

        @block.gpsimd
        def _(pool):
            def inverse_deviation(slot, mv_ready, added, rstd_ready, n):
                pool.wait_ge(mv_ready, n + 1)
                nc.gpsimd.tensor_scalar(ln_var[:, slot, :], ln_mv[:, slot, :, 1], EPS, None, ALU.add).then_inc(added, 1)
                pool.wait_ge(added, n + 1)
                nc.gpsimd.tensor_tensor(ln_rstd[:, slot, :], ln_var[:, slot, :], minus_half[:],
                                        ALU.pow).then_inc(rstd_ready, 1)

            nc.gpsimd.memset(minus_half[:], -0.5).then_inc(s["half_ready"], 1)
            pool.wait_ge(s["half_ready"], 1)
            nc.gpsimd.memset(ident[:], 0.0).then_inc(s["const_ready"], 1)
            pool.wait_ge(s["const_ready"], 1)
            nc.gpsimd.affine_select(out=ident[:], in_=ident[:], compare_op=ALU.not_equal, fill=1.0, base=0,
                                    pattern=[[-1, P]], channel_multiplier=1).then_inc(s["const_ready"], 1)
            nc.gpsimd.memset(ones[:], 1.0).then_inc(s["const_ready"], 1)
            pool.wait_ge(s["const_ready"], 3)
            for b in range(B):
                if b:
                    pool.wait_ge(s["ones_row"], b)
                nc.gpsimd.memset(k_low[b][HD:HD + 1, :, :].bitcast(F32), 1.0).then_inc(s["ones_row"], 1)
            pool.wait_ge(s["ones_row"], B)
            for g in range(NG):
                inverse_deviation(g % 2, s["mv_done"], s["eps_added"], s["rstd_done"], g)
            for c in range(NC):
                pool_split(pool, (0, 0), "K", c)
            for c in range(NC):
                pool_split(pool, (0, 0), "Q", c)
            units("pool", pool, pool_unit)
            for g in range(NG + 1):
                if g < NG:
                    inverse_deviation(0, f["f_mv1"], f["f_ep1"], f["f_rs1"], g)
                    inverse_deviation(0, f["f_mv2"], f["f_ep2"], f["f_rs2"], g)
                if g >= 1:
                    inverse_deviation(1, f["f_mv3"], f["f_ep3"], f["f_rs3"], g - 1)

        @block.scalar
        def _(act):
            for g in range(NG):
                act.wait_ge(s["xnT_ps_ready"], g + 1)
                nc.scalar.activation(xnT[:, g * CH:(g + 1) * CH], o_ps[g % 2][:], ACT.Copy).then_inc(s["xnT_done"], 1)
            first = (0, 0)
            for _, kind, c in PREP:
                if kind in "KQ":
                    act_evac(act, first, kind, c)
                if kind == "Q" and c < NC - 1:
                    act_evac(act, first, "M", c)
            units("act", act, act_unit)
            act_denom(act, (PAIRS - 1, B - 1), NC - 1)
            for g in range(NG):
                j = g % 2
                act.wait_ge(f["f_xT_ps"], g + 1)
                if g >= 2:
                    act.wait_ge(f["f_p_ps"], g - 1)
                nc.scalar.activation(xnT2[j], score_ps[0][:], ACT.Copy).then_inc(f["f_xT"], 1)
                act.wait_ge(f["f_p_ps"], g + 1)
                if g >= 2:
                    act.wait_ge(f["f_h_ps"], (g - 1) * (FF // P))
                nc.scalar.activation(pT[j], score_ps[1][0:RANK, :], ACT.Copy).then_inc(f["f_p"], 1)
                if g == 0:
                    act.wait_ge(f["ffn_w_in"], 6 * 16)
                for k in range(FF // P):
                    act.wait_ge(f["f_h_ps"], g * (FF // P) + k + 1)
                    if g >= 1 and k == 0:
                        act.wait_ge(f["f_q_ps"], g)
                    nc.scalar.activation(hT[:, k, :], (work[:2] + o_ps)[k][:], ACT.Gelu_apprx_tanh,
                                         bias=b1c[:, k:k + 1]).then_inc(f["f_h"], 1)
                act.wait_ge(f["f_q_ps"], g + 1)
                if g >= 2:
                    act.wait_ge(f["f_z_ps"], g - 1)
                nc.scalar.activation(qT[j], work[2][0:RANK, :], ACT.Copy).then_inc(f["f_q"], 1)

        @block.vector
        def _(dve):
            ln_count = {}

            def layer_norm(tiles, outs, slot, S1, S2, S3, SO, n):
                for t in range(TC):
                    ins = nc.vector.bn_stats(ln_stats[:, slot, t, :], tiles[t])
                ins.then_inc(S1, 1)
                dve.wait_ge(S1, n + 1)
                for t in range(TC):
                    ins = nc.vector.bn_aggr(ln_mv[:, slot, t, :], ln_stats[:, slot, t, :])
                ins.then_inc(S2, 1)
                dve.wait_ge(S2, n + 1)
                dve.wait_ge(S3, n + 1)
                for t in range(TC):
                    ins = nc.vector.tensor_scalar(outs[t], tiles[t], ln_mv[:, slot, t, 0:1],
                                                  ln_rstd[:, slot, t:t + 1], ALU.subtract, ALU.mult)
                    ins.then_inc(SO, 1)

            for g in range(NG):
                j = g % 2
                dve.wait_ge(s[f"x_in{j}"], 16 * (g // 2 + 1))
                if g >= 2:
                    dve.wait_ge(s["xnT_ps_ready"], g - 1)
                layer_norm([xg[:, j, t, :] for t in range(TC)], [xn[:, j, t, :] for t in range(TC)], j,
                           s["stats_done"], s["mv_done"], s["rstd_done"], s["xn_done"], g)
            dve.wait_ge(s["y_init"], 16)
            nc.vector.tensor_copy(y_acc[:, 1:B * T, :], y_acc[:, 0:1, :].to_broadcast([P, B * T - 1, D])).then_inc(s["y_init"], 16)
            first = (0, 0)
            for _, kind, c in PREP:
                if kind == "V":
                    dve_v(dve, first, c, None)
                if kind == "Q":
                    for r in range(TC * NC * c, TC * NC * (c + 1)):
                        dve_max(dve, first, r)
                    if c < NC - 1:
                        dve_neg_max(dve, first, c)
            units("dve", dve, dve_unit)
            u = (PAIRS - 1, B - 1)
            add_tile(dve, u, STEPS - 1, DVE_TILES, s["dve_sum_done"], dve_sum)
            dve_tail(dve, u, NC - 1, SUM_AT)
            dve_tail(dve, u, NC - 1, RECIP_AT)
            dve_tail(dve, u, NC - 1, NORM_AT)
            dve_tail(dve, u, NC - 1, Y_AT)
            dve.wait_ge(s["y_done"], end)
            for g in range(NG + 1):
                if g < NG:
                    j = g % 2
                    yt = y_acc[:, g * TC:(g + 1) * TC, :]
                    layer_norm([yt[:, t, :] for t in range(TC)], [yt[:, t, :] for t in range(TC)], 0,
                               f["f_st1"], f["f_mv1"], f["f_rs1"], f["f_yn"], g)
                    dve.wait_ge(f["f_yn"], TC * (g + 1))
                    dve.wait_ge(g_in[j], 16 * (g // 2 + 1))
                    nc.vector.tensor_tensor(x1[:, g % 4], yt, xg[:, j], ALU.add).then_inc(f["f_x1"], 1)
                    dve.wait_ge(f["f_x1"], g + 1)
                    if g >= 2:
                        dve.wait_ge(f["f_xT_ps"], g - 1)
                    layer_norm([x1[:, g % 4, t, :] for t in range(TC)], [xn[:, j, t, :] for t in range(TC)], 0,
                               f["f_st2"], f["f_mv2"], f["f_rs2"], f["f_xn"], g)
                if g >= 1:
                    e = g - 1
                    j = e % 2
                    dve.wait_ge(f["f_z_ps"], e + 1)
                    if e == 0:
                        dve.wait_ge(f["ffn_w_in"], 6 * 16)
                    if e >= 2:
                        dve.wait_ge(out_dma[j], 16 * (e // 2))
                    nc.vector.tensor_tensor(z[j], work[3][:].rearrange("p (t d) -> p t d", t=TC),
                                            b2r.unsqueeze(1).to_broadcast([P, TC, D]), ALU.add).then_inc(f["f_z"], 1)
                    dve.wait_ge(f["f_z"], e + 1)
                    layer_norm([z[j][:, t, :] for t in range(TC)], [z[j][:, t, :] for t in range(TC)], 1,
                               f["f_st3"], f["f_mv3"], f["f_rs3"], f["f_zn"], e)
                    dve.wait_ge(f["f_zn"], TC * (e + 1))
                    nc.vector.tensor_tensor(z[j], z[j], x1[:, e % 4], ALU.add).then_inc(f["f_out"], 1)

        @block.tensor
        def _(pe):
            pe.wait_ge(s["const_ready"], 3)
            for g in range(NG):
                pe.wait_ge(s["xn_done"], TC * (g + 1))
                if g >= 2:
                    pe.wait_ge(s["xnT_done"], g - 1)
                for t in range(TC):
                    last = nc.tensor.transpose(o_ps[g % 2][:, t * P:(t + 1) * P], xn[:, g % 2, t, :], ident[:])
                last.then_inc(s["xnT_ps_ready"], 1)
            pe.wait_ge(s["xnT_done"], NG)
            me = Pe(pe)
            me.prepare_alone((0, 0))
            units("pe", pe, lambda _, u, before, last=False: me.unit(u, before, last))
            u = (PAIRS - 1, B - 1)
            me.values(u, STEPS - 1)
            me.denominators(u, NC - 1)
            me.out_projection(u, NC - 1)
            pe.wait_ge(f["ffn_w_in"], 6 * 16)
            for g in range(NG):
                j = g % 2
                pe.wait_ge(f["f_xn"], TC * (g + 1))
                if g >= 1:
                    pe.wait_ge(f["f_xT"], g)
                for t in range(TC):
                    last = nc.tensor.transpose(score_ps[0][:, t * P:(t + 1) * P], xn[:, j, t, :], ident[:])
                last.then_inc(f["f_xT_ps"], 1)
                pe.wait_ge(f["f_xT"], g + 1)
                if g >= 1:
                    pe.wait_ge(f["f_p"], g)
                nc.tensor.matmul(score_ps[1][0:RANK, :], u1, xnT2[j], start=True, stop=True).then_inc(f["f_p_ps"], 1)
                pe.wait_ge(f["f_p"], g + 1)
                for k in range(FF // P):
                    if g >= 1:
                        pe.wait_ge(f["f_h"], (g - 1) * (FF // P) + k + 1)
                    nc.tensor.matmul((work[:2] + o_ps)[k][:], v1[:, k * P:(k + 1) * P], pT[j],
                                     start=True, stop=True).then_inc(f["f_h_ps"], 1)
                if g >= 1:
                    pe.wait_ge(f["f_q"], g)
                for k in range(FF // P):
                    pe.wait_ge(f["f_h"], g * (FF // P) + k + 1)
                    last = nc.tensor.matmul(work[2][0:RANK, :], u2[:, k, :], hT[:, k, :],
                                            start=(k == 0), stop=(k == FF // P - 1))
                last.then_inc(f["f_q_ps"], 1)
                pe.wait_ge(f["f_q"], g + 1)
                if g >= 1:
                    pe.wait_ge(f["f_z"], g)
                else:
                    pe.wait_ge(s["y_done"], end)
                for t in range(TC):
                    last = nc.tensor.matmul(work[3][:, t * D:(t + 1) * D], qT[j][:, t * P:(t + 1) * P], v2,
                                            start=True, stop=True)
                last.then_inc(f["f_z_ps"], 1)


_INS = ['L0_attn_x', 'L0_attn_Wq', 'L0_attn_bq', 'L0_attn_Wk', 'L0_attn_bk', 'L0_attn_Wv', 'L0_attn_bv',
        'L0_attn_Wo', 'L0_attn_bo', 'L0_ffn_U1', 'L0_ffn_V1', 'L0_ffn_b1', 'L0_ffn_U2', 'L0_ffn_V2', 'L0_ffn_b2']


def kernel(**inputs):
    import numpy as _np
    import concourse.bacc as _bacc
    from concourse import mybir as _mybir
    from concourse.bass_utils import run_bass_kernel_spmd as _run

    nc = _bacc.Bacc("TRN2", target_bir_lowering=False, num_devices=1)
    arrays, args = {}, []
    for name in _INS:
        a = _np.ascontiguousarray(inputs[name])
        arrays[f"in_{name}"] = a
        args.append(nc.dram_tensor(f"in_{name}", a.shape, _mybir.dt.from_np(a.dtype), kind="ExternalInput").ap())
    x = arrays["in_L0_attn_x"]
    args.append(nc.dram_tensor("block_out", x.shape, _mybir.dt.from_np(x.dtype), kind="ExternalOutput").ap())
    build(nc, *args)
    return _run(nc, [arrays], core_ids=[0]).results[0]["block_out"]
```

```python
import concourse.bass as bass
from concourse import mybir
from contextlib import ExitStack

F32 = mybir.dt.float32
F32R = mybir.dt.float32r
ALU = mybir.AluOpType
ACT = mybir.ActivationFunctionType
AX = mybir.AxisListType

P = 128
B, S, D = 2, 2048, 128
H, HD = 16, 64
FF, RANK = 512, 32
EPS = 1e-5
PAIRS = H // 2
T = S // P
CH = 512
NC = S // CH
TC = CH // P
STEPS = NC * T
PRING = 4
SCALE = float(HD) ** -0.5

SCORE_N = 2 * STEPS
PV_N = STEPS
MAXN = 2 * TC * NC * NC
DVE_TILES = [0, 2, 5, 8, 11, 15]
POOL_TILES = [t for t in range(T) if t not in DVE_TILES]
DVE_ADDS, POOL_ADDS = len(DVE_TILES) - 1, len(POOL_TILES) - 1
DVE_SUM_N, POOL_SUM_N = NC * DVE_ADDS, NC * POOL_ADDS
TAIL_DMA_N = NC * 2 * 16
KQ_N = 2 * NC
KQ_DMA_N = 6 * 16 * NC // 2
M_DMA_N = 2 * 16 * NC // 2

W_DMA_N = 6 * 16 // B
WO_DMA_N = 16 // B
UNIT_COUNTS = sorted({SCORE_N, PV_N, MAXN, DVE_SUM_N, POOL_SUM_N, TAIL_DMA_N, NC * 16, KQ_N, KQ_DMA_N, M_DMA_N, NC, W_DMA_N, WO_DMA_N})

K_AT = [0, 1, 5, 6]
V_AT = [7, 9, 10, 15]
Q_AT = [8, 18, 30, 44]
PAIRS_OF_MAX = TC * NC * NC
MAX_FIRST = 11


def max_step(r):
    return MAX_FIRST + r * (STEPS - MAX_FIRST) // PAIRS_OF_MAX


M_LAG = 4
M_AT = [max_step(TC * NC * (c + 1) - 1) + M_LAG for c in range(NC)]
M_LATE = M_AT[-1] - STEPS


def prep_order(k_at, v_at, q_at, m_at):
    ops = [(k_at[c], "K", c) for c in range(NC)] + [(v_at[c], "V", c) for c in range(NC)]
    ops += [(q_at[c], "Q", c) for c in range(NC)] + [(m_at[c], "M", c) for c in range(NC - 1)]
    return sorted(ops)


PREP = prep_order(K_AT, V_AT, Q_AT, M_AT)

OWN_Q_AT = [None, 0, 5, 11]
OWN_M_AT = [None, 11, 19, 27]
FIRST_K_AT, FIRST_V_AT, FIRST_Q_AT = [13, 15, 18, 20], [20, 21, 24, 25], [24, 34, 43, 52]
FIRST_MAX = 26


def first_max_step(r):
    return FIRST_MAX + r * (STEPS - FIRST_MAX) // PAIRS_OF_MAX


FIRST_M_AT = [first_max_step(TC * NC * (c + 1) - 1) + M_LAG for c in range(NC)]
assert FIRST_M_AT[-1] - STEPS <= M_LATE
FIRST_PREP = prep_order(FIRST_K_AT, FIRST_V_AT, FIRST_Q_AT, FIRST_M_AT)


def step_pairs(st, first=False):
    if not first:
        return [(r, "next") for r in range(PAIRS_OF_MAX) if max_step(r) == st]
    own = [(r, "this") for r in range(TC * NC, PAIRS_OF_MAX) if 1 + (r - TC * NC) // 2 == st]
    return own + [(r, "next") for r in range(PAIRS_OF_MAX) if first_max_step(r) == st]


def step_preps(st, first=False):
    if not first:
        return [(kind, c, "next") for at_step, kind, c in PREP if at_step == st] \
            + [("M", NC - 1, "this")] * (st == M_LATE)
    own = [("Q", c, "this") for c in range(1, NC) if OWN_Q_AT[c] == st]
    own += [("M", c, "this") for c in range(1, NC) if OWN_M_AT[c] == st]
    return own + [(kind, c, "next") for at_step, kind, c in FIRST_PREP if at_step == st]


SUM_AT, DENOM_AT, RECIP_AT, NORM_AT, WO_AT, Y_AT = 2, 3, 9, 12, 13, 14
WORK_BANKS = 4


START = [("x", g) for g in range(NC + 1)] + [("K", 0), ("x", 5), ("K", 1), ("x", 6), ("K", 2), ("x", 7), ("K", 3)]

START_POOL = [("x", g) for g in range(NC + 2)] + [("K", 0), ("x", 6), ("K", 1), ("x", 7), ("K", 2), ("K", 3)]


def step_uses(st, first=False):
    c, kt = st // T, st % T
    done = (c - 1, "this") if c else (NC - 1, "before")
    uses = [("max", 2 * r + h, whose) for r, whose in step_pairs(st, first) for h in range(2)]
    if kt == DENOM_AT:
        uses.append(("L", *done))
    if kt == WO_AT:
        uses.append(("Wo", *done))
    return uses + step_preps(st, first)


UNIT_USES = [use for st in range(STEPS) for use in step_uses(st)]
assert len(UNIT_USES) % WORK_BANKS == 0
BANK = {(kind, n): k % WORK_BANKS for k, (kind, n, _) in enumerate(UNIT_USES)}

NG = B * NC
GROUP_AT = [4, 12, 20, 28, 36, 50, 64, 67]
FFN_AT = dict(norm1=0, x1=2, norm2=4, xT=6, p=7, low=7, h=8, q=9, z=10, norm3=11, out=13)
END_SUM, END_DENOM, END_NORM, END_Y = STEPS, STEPS, STEPS + 1, STEPS + 2
LAST_STEPS = GROUP_AT[-1] + FFN_AT["out"] + 1
assert all(GROUP_AT[NC + c] > (c + 1) * T + Y_AT for c in range(NC - 1)) and GROUP_AT[-1] > END_Y
FFN_BANK = dict(xT=2, p=3, h0=0, h1=1, h2=2, h3=3, q=0, z=1)
SPLIT = 3 * RANK


def ffn_at(st, *stages):
    return [(stage, g) for g in range(NG) for stage in stages if GROUP_AT[g] + FFN_AT[stage] == st]



def build(nc, x, Wq, bq, Wk, bk, Wv, bv, Wo, bo, U1, V1, b1, U2, V2, b2, out):
    x_v = x.rearrange("b (t p) d -> p (b t) d", p=P)
    out_v = out.rearrange("b (t p) d -> p (b t) d", p=P)
    wq_v = Wq.rearrange("d (i h) k -> i d (h k)", h=2)
    wk_v = Wk.rearrange("d (i h) k -> i d (h k)", h=2)
    wv_v = Wv.rearrange("d (i h) k -> i d (h k)", h=2)
    wo_v = Wo.rearrange("(i h) k m -> i (h k) m", h=2)
    bq_v = bq.rearrange("(i h) k -> i (h k)", h=2)
    bk_v = bk.rearrange("(i h) k -> i (h k)", h=2)
    bv_v = bv.rearrange("(i h) k -> i (h k)", h=2)

    ctx = ExitStack()
    with ctx:
        def sb(name, shape, dt=F32):
            return ctx.enter_context(nc.sbuf_tensor(name, shape, dt))

        def sem(name):
            return ctx.enter_context(nc.semaphore(name))

        ident = sb("ident", [P, P])
        ones = sb("ones", [P, HD])
        xnT = sb("xnT", [P, B * S])
        y_acc = sb("y_acc", [P, B * T, D])
        w_qkv = sb("w_qkv", [P, 3, P])
        b_qk = sb("b_qk", [P, 2])
        b_v = sb("b_v", [P, P])
        w_o = sb("w_o", [P, D])
        k_low = [sb(f"k_low{b}", [HD + 1, 2, S], F32R) for b in range(B)]
        q_split = sb("q_split", [P, 2, S], F32R)
        q_max = sb("q_max", [HD + 1, 2, S], F32R)
        v_sb = [sb(f"v_sb{b}", [P, T, P]) for b in range(B)]
        kq_f32 = sb("kq_f32", [P, 2, CH])
        q_hi = sb("q_hi", [P, 2, CH], F32R)
        q_lo = sb("q_lo", [P, 2, CH], F32R)
        probs = sb("probs", [P, PRING, 2, CH])
        dve_sum = sb("dve_sum", [P, 2, CH])
        pool_sum = sb("pool_sum", [P, 2, CH])
        sum_all = sb("sum_all", [P, 2, CH])
        denom = sb("denom", [P, CH])
        denom_col = sb("denom_col", [P, CH // HD])
        o_norm = sb("o_norm", [P, CH])
        max_part = sb("max_part", [P, 2, 2 * TC, NC])
        neg_max = sb("neg_max", [P, 2, 2 * TC])
        max_rows = sb("max_rows", [2 * TC, 2, P], F32R)
        ln_stats = sb("ln_stats", [P, 3, TC, 6])
        ln_mv = sb("ln_mv", [P, 3, TC, 2])
        ln_rstd = sb("ln_rstd", [P, 3, TC])
        ln_var = sb("ln_var", [P, 3, TC])
        minus_half = sb("minus_half", [P, TC])

        xg = sb("xg", [P, 2, TC, D])
        k_dup1 = sb("k_dup1", [P, 2, S], F32R)
        with ExitStack() as shared:
            k_dup0 = shared.enter_context(nc.sbuf_tensor("k_dup0", [P, 2, S], F32R))
            k_hi = shared.enter_context(nc.sbuf_tensor("k_hi", [P, 2, CH], F32R))
            k_lo = shared.enter_context(nc.sbuf_tensor("k_lo", [P, 2, CH], F32R))
        k_dup = [k_dup0, k_dup1]
        v1_split = sb("v1_split", [SPLIT, FF], F32R)
        p_split = sb("p_split", [SPLIT, 2, CH], F32R)
        v1_f32 = sb("v1_f32", [SPLIT, FF])
        u1 = sb("u1", [P, SPLIT])
        b1c = sb("b1c", [P, FF // P])
        u2 = sb("u2", [P, FF // P, RANK])
        v2 = sb("v2", [P, D])
        b2r = sb("b2r", [P, D])
        xn = sb("xn", [P, 2, TC, D])
        xnT2 = sb("xnT2", [P, 2, CH])
        q_parts = sb("q_parts", [P, 2, CH])

        denom_dram = nc.dram_tensor("denom_scratch", (2, CH), F32, kind="Internal").ap()

        def bank(name):
            return ctx.enter_context(nc.psum_tensor(name, [P, CH], F32))

        score_ps = [bank(f"score_ps{h}") for h in range(2)]
        work = [bank(f"work{n}") for n in range(WORK_BANKS)]
        o_ps = [bank(f"o_ps{n}") for n in range(2)]

        names = """half_ready eps_added const_ready x_in0 x_in1 x_late0 x_late1 stats_done mv_done rstd_done xn_done xnT_ps_ready xnT_done y_init
            w_in wo_in k_ps q_ps v_ps m_ps kq_evac kq_hi_done kq_split v_done
            m_evac k_dma0 k_dma1 q_dma0 q_dma1 m_dma0 m_dma1 ones_row
            score_ready exp_done pv_done dve_sum_done pool_sum_done recip_done denom_copied col_dma scratch_dma denom_dma sum_all_done
            denom_ps_ready denom_done o_norm_done wo_ps_ready y_done max_ready max_done neg_max_done""".split()
        s = {n: sem(n) for n in names}
        k_dma, q_dma, m_dma = ([s[f"{n}_dma{j}"] for j in range(2)] for n in "kqm")

        class Pair:

            def __init__(self, eng, number, base, spare, shift=0):
                self.eng, self.number, self.base, self.spare, self.shift = eng, number, base, spare, shift

            def __add__(self, n):
                return Pair(self.eng, self.number, self.base, self.spare, self.shift + n)

            def __sub__(self, n):
                return self + -n

        def at(unit, per_unit, n):
            i, b = unit
            n += b * per_unit
            if isinstance(i, int):
                return i * B * per_unit + n
            n += i.shift * B * per_unit
            if n == 0:
                return i.base[per_unit]
            spare = i.spare.pop(0)
            i.spare.append(spare)
            i.eng.reg_add(spare, i.base[per_unit], n)
            return spare

        def number(i):
            return i if isinstance(i, int) else i.number + i.shift

        def is_first(unit):
            return isinstance(unit[0], int) and unit == (0, 0)

        def following(unit):
            i, b = unit
            return (i, 1) if b == 0 else (i + 1, 0)


        class Pe:

            def __init__(self, pe):
                self.pe = pe
                self.user = {}

            def take(self, kind, n, unit):
                bank = FFN_BANK[kind] if kind in FFN_BANK else BANK[kind, n]
                if bank in self.user:
                    was, k, w = self.user[bank]
                    if was == "max":
                        self.pe.wait_ge(s["max_done"], at(w, MAXN, k + 1))
                    elif was in "KQ":
                        self.pe.wait_ge(s["kq_evac"], at(w, KQ_N, k + 1 + (NC if was == "Q" else 0)))
                    elif was == "V":
                        self.pe.wait_ge(s["v_done"], at(w, NC, k + 1))
                    elif was == "M":
                        self.pe.wait_ge(s["m_evac"], at(w, NC, k + 1))
                    elif was == "L":
                        self.pe.wait_ge(s["denom_copied"], at(w, NC, k + 1))
                    elif was == "Wo":
                        self.pe.wait_ge(s["y_done"], at(w, NC, k + 1))
                    elif was[0] == "h":
                        self.pe.wait_ge(f["f_h"], k * (FF // P) + int(was[1]) + 1)
                    else:
                        self.pe.wait_ge(f[{"xT": "f_xT", "p": "f_low", "q": "f_q", "z": "f_z"}[was]], k + 1)
                self.user[bank] = (kind, n, unit)
                return work[bank]

            def project(self, v, kind, c):
                pe, b = self.pe, v[1]
                proj_ps = self.take(kind, c, v)
                cols = slice(b * S + c * CH, b * S + (c + 1) * CH)
                if kind == "K":
                    if c == 0:
                        pe.wait_ge(s["w_in"], at((v[0], 0), W_DMA_N, 6 * 16))
                    nc.tensor.matmul(proj_ps[:], w_qkv[:, 1, :], xnT[:, cols],
                                     start=True, stop=True).then_inc(s["k_ps"], 1)
                elif kind == "Q":
                    nc.tensor.matmul(proj_ps[:], w_qkv[:, 0, :], xnT[:, cols],
                                     start=True, stop=True).then_inc(s["q_ps"], 1)
                elif kind == "V":
                    for t in range(TC):
                        at0 = b * S + c * CH + t * P
                        last = nc.tensor.matmul(proj_ps[:, t * P:(t + 1) * P], xnT[:, at0:at0 + P],
                                                w_qkv[:, 2, :], start=True, stop=True)
                    last.then_inc(s["v_ps"], 1)
                else:
                    pe.wait_ge(s["neg_max_done"], at(v, NC, c + 1))
                    nc.tensor.matmul(proj_ps[0:2 * TC, 0:P], neg_max[:, c % 2, :], ident[:],
                                     start=True, stop=True).then_inc(s["m_ps"], 1)

            def max_pair(self, v, r):
                pe, b = self.pe, v[1]
                c, qt, kc = r // (TC * NC), r // NC % TC, r % NC
                if qt == 0 and kc == 0:
                    pe.wait_ge(s["kq_hi_done"], at(v, KQ_N, NC + c + 1))
                if r < NC:
                    pe.wait_ge(k_dma[kc % 2], at(v, KQ_DMA_N, 6 * 16 * (kc // 2 + 1)))
                for h in range(2):
                    max_ps = self.take("max", 2 * r + h, v)
                    rows = slice(h * HD, (h + 1) * HD)
                    nc.tensor.matmul(max_ps[:], q_hi[rows, c % 2, qt * P:(qt + 1) * P],
                                     k_dup[b][rows, h, kc * CH:(kc + 1) * CH],
                                     start=True, stop=True).then_inc(s["max_ready"], 1)

            def scores(self, u, st):
                pe, b = self.pe, u[1]
                c, kt = st // T, st % T
                cols, keys = slice(c * CH, (c + 1) * CH), slice(kt * P, (kt + 1) * P)
                if kt == 0:
                    pe.wait_ge(q_dma[c % 2], at(u, KQ_DMA_N, 6 * 16 * (c // 2 + 1)))
                    pe.wait_ge(m_dma[c % 2], at(u, M_DMA_N, 2 * 16 * (c // 2 + 1)))
                if st == 0 and is_first(u):
                    pe.wait_ge(s["ones_row"], 2)
                for h in range(2):
                    n = 2 * st + h
                    if not (is_first(u) and n < 2):
                        pe.wait_ge(s["exp_done"], at(u, SCORE_N, n - 1))
                    nc.tensor.matmul(score_ps[h][:], k_dup[b][:, h, keys], q_split[:, h, cols],
                                     start=True, stop=False)
                    nc.tensor.matmul(score_ps[h][:], k_low[b][:, h, keys], q_max[:, h, cols],
                                     start=False, stop=True).then_inc(s["score_ready"], 1)

            def values(self, u, st):
                pe, b = self.pe, u[1]
                c, kt = st // T, st % T
                if kt == 0 and not (is_first(u) and c < 2):
                    pe.wait_ge(s["o_norm_done"], at(u, NC, c - 1))
                if st == 0:
                    pe.wait_ge(s["v_done"], at(u, NC, NC))
                for h in range(2):
                    pe.wait_ge(s["exp_done"], at(u, SCORE_N, 2 * st + h + 1))
                    last = nc.tensor.matmul(o_ps[c % 2][h * HD:(h + 1) * HD, :],
                                            v_sb[b][:, kt, h * HD:(h + 1) * HD],
                                            probs[:, st % PRING, h, :],
                                            start=(kt == 0), stop=(kt == T - 1))
                last.then_inc(s["pv_done"], 1)

            def denominators(self, u, c):
                pe = self.pe
                pe.wait_ge(s["sum_all_done"], at(u, NC, c + 1))
                tail_ps = self.take("L", c, u)
                for h in range(2):
                    last = nc.tensor.matmul(tail_ps[h * HD:(h + 1) * HD, :], ones[:], sum_all[:, h, :],
                                            start=True, stop=True)
                last.then_inc(s["denom_ps_ready"], 1)

            def out_projection(self, u, c):
                pe = self.pe
                pe.wait_ge(s["o_norm_done"], at(u, NC, c + 1))
                if c == 0 and u[1] == 0:
                    pe.wait_ge(s["wo_in"], at(u, WO_DMA_N, 16))
                tail_ps = self.take("Wo", c, u)
                for t in range(TC):
                    last = nc.tensor.matmul(tail_ps[:, t * D:(t + 1) * D], o_norm[:, t * P:(t + 1) * P],
                                            w_o[:], start=True, stop=True)
                last.then_inc(s["wo_ps_ready"], 1)

            def prepare_alone(self, v):
                self.project(v, "Q", 0)
                for c in range(NC):
                    self.project(v, "V", c)
                for r in range(TC * NC):
                    self.max_pair(v, r)
                self.project(v, "M", 0)

            def unit(self, u, before, last=False):
                whose = {"before": before, "this": u, "next": None if last else following(u)}
                first = is_first(u)
                if before is not None and not is_first(before):
                    ended = {"this": before, "next": u}
                    for kind, n, who in UNIT_USES[-WORK_BANKS:]:
                        self.user[BANK[kind, n]] = (kind, n, ended[who])
                for st in range(STEPS):
                    self.scores(u, st)
                    uses = [(kind, n, whose[who]) for kind, n, who in step_uses(st, first) if whose[who] is not None]
                    pairs = [(w, n // 2) for kind, n, w in uses if kind == "max" and n % 2 == 0]
                    for w, r in pairs[:1]:
                        self.max_pair(w, r)
                    if st:
                        self.values(u, st - 1)
                    elif before is not None:
                        self.values(before, STEPS - 1)
                    for w, r in pairs[1:]:
                        self.max_pair(w, r)
                    for kind, n, unit in uses:
                        if kind == "L":
                            self.denominators(unit, n)
                        elif kind == "Wo":
                            self.out_projection(unit, n)
                        elif kind != "max":
                            self.project(unit, kind, n)
                    if last:
                        self.ffn(st)
                if last:
                    for st in range(STEPS, LAST_STEPS):
                        if st == STEPS:
                            self.values(u, STEPS - 1)
                        if st == END_DENOM:
                            self.denominators(u, NC - 1)
                        if st == END_NORM:
                            self.out_projection(u, NC - 1)
                        self.ffn(st)

            def ffn(self, st):
                pe = self.pe
                for stage, g in ffn_at(st, "xT", "p", "h", "q", "z"):
                    j = g % 2
                    if stage == "xT":
                        pe.wait_ge(f["f_xn"], TC * (g + 1))
                        ps = self.take("xT", g, None)
                        for t in range(TC):
                            last = nc.tensor.transpose(ps[:, t * P:(t + 1) * P], xn[:, j, t, :], ident[:])
                        last.then_inc(f["f_xT_ps"], 1)
                    elif stage == "p":
                        if g == 0:
                            pe.wait_ge(f["ffn_w_in"], FFN_W_N)
                        pe.wait_ge(f["f_xT"], g + 1)
                        ps = self.take("p", g, None)
                        nc.tensor.matmul(ps[0:SPLIT, :], u1[:], xnT2[:, j, :], start=True, stop=True).then_inc(f["f_p_ps"], 1)
                    elif stage == "h":
                        if g == 0:
                            pe.wait_ge(f["v1_split"], 2)
                        pe.wait_ge(f["f_low"], g + 1)
                        for k in range(FF // P):
                            ps = self.take(f"h{k}", g, None)
                            nc.tensor.matmul(ps[:], v1_split[:, k * P:(k + 1) * P], pT[j],
                                             start=True, stop=True).then_inc(f["f_h_ps"], 1)
                    elif stage == "q":
                        ps = self.take("q", g, None)
                        for k in range(FF // P):
                            pe.wait_ge(f["f_h"], g * (FF // P) + k + 1)
                            last = nc.tensor.matmul(ps[k * RANK:(k + 1) * RANK, :], u2[:, k, :], hT[:, k, :],
                                                    start=True, stop=True)
                        last.then_inc(f["f_q_ps"], 1)
                    else:
                        pe.wait_ge(f["f_q"], g + 1)
                        ps = self.take("z", g, None)
                        for t in range(TC):
                            last = nc.tensor.matmul(ps[:, t * D:(t + 1) * D], q_parts[:, j, t * P:(t + 1) * P], v2[:],
                                                    start=True, stop=True)
                        last.then_inc(f["f_z_ps"], 1)

        def act_evac(act, v, kind, c):
            proj_ps = work[BANK[kind, c]] if kind != "V" else None
            if kind in "KQ":
                n = c + (NC if kind == "Q" else 0)
                act.wait_ge(s["k_ps" if kind == "K" else "q_ps"], at(v, NC, c + 1))
                if not (is_first(v) and n < 2):
                    act.wait_ge(s["kq_split"], at(v, KQ_N, n - 1))
                j = 1 if kind == "K" else 0
                hi = k_hi if kind == "K" else q_hi
                if not (is_first(v) and c < 2):
                    dma = k_dma if kind == "K" else q_dma
                    act.wait_ge(dma[c % 2], at(v, KQ_DMA_N, 6 * 16 * (c // 2)))
                    if kind == "Q":
                        act.wait_ge(s["max_ready"], at(v, MAXN, 2 * TC * NC * (c - 1)))
                nc.scalar.activation(hi[:, c % 2, :], proj_ps[:], ACT.Identity,
                                     bias=b_qk[:, j:j + 1]).then_inc(s["kq_hi_done"], 1)
                nc.scalar.activation(kq_f32[:, n % 2, :], proj_ps[:], ACT.Identity,
                                     bias=b_qk[:, j:j + 1]).then_inc(s["kq_evac"], 1)
            elif kind == "M":
                act.wait_ge(s["m_ps"], at(v, NC, c + 1))
                if not (is_first(v) and c < 2):
                    act.wait_ge(m_dma[c % 2], at(v, M_DMA_N, 2 * 16 * (c // 2)))
                nc.scalar.activation(max_rows[:, c % 2, :], proj_ps[0:2 * TC, 0:P],
                                     ACT.Copy).then_inc(s["m_evac"], 1)

        def act_denom(act, u, c):
            act.wait_ge(s["denom_ps_ready"], at(u, NC, c + 1))
            if not (is_first(u) and c == 0):
                act.wait_ge(s["o_norm_done"], at(u, NC, c))
            nc.scalar.activation(denom[:], work[BANK["L", c]][:], ACT.Copy).then_inc(s["denom_copied"], 1)

        def act_unit(act, u, before, last=False):
            v = following(u)
            for st in range(STEPS):
                for h in range(2):
                    act.wait_ge(s["score_ready"], at(u, SCORE_N, 2 * st + h + 1))
                    if h == 0 and not (is_first(u) and st < PRING):
                        act.wait_ge(s["pv_done"], at(u, PV_N, st - PRING + 1))
                        if st >= PRING or before is not None:
                            w, ws = (u, st - PRING) if st >= PRING else (before, st - PRING + STEPS)
                            wc, wk = ws // T, ws % T
                            if wk in DVE_TILES:
                                act.wait_ge(s["dve_sum_done"], at(w, DVE_SUM_N, wc * DVE_ADDS + max(DVE_TILES.index(wk), 1)))
                            else:
                                act.wait_ge(s["pool_sum_done"], at(w, POOL_SUM_N, wc * POOL_ADDS + max(POOL_TILES.index(wk), 1)))
                    nc.scalar.activation(probs[:, st % PRING, h, :], score_ps[h][:], ACT.Exp,
                                         scale=SCALE).then_inc(s["exp_done"], 1)
                done = (u, st // T - 1) if st >= T else (before, NC - 1)
                if done[0] is not None and st % T == DENOM_AT:
                    act_denom(act, *done)
                for kind, pc, who in step_preps(st, is_first(u)):
                    if who == "this" or not last:
                        act_evac(act, u if who == "this" else v, kind, pc)
                if last:
                    act_ffn(act, u, st)
            if last:
                for st in range(STEPS, LAST_STEPS):
                    act_ffn(act, u, st)

        def act_ffn(act, u, st):
            for stage, g in ffn_at(st, "xT", "p", "h", "q"):
                j = g % 2
                if stage == "xT":
                    if g == 0:
                        for slot in range(2):
                            act.wait_ge(k_dma[slot], at(u, KQ_DMA_N, KQ_DMA_N))
                        act.wait_ge(f["ffn_w_in"], FFN_W_N)
                        nc.scalar.activation(v1_split[:], v1_f32[:], ACT.Copy).then_inc(f["v1_high"], 1)
                    act.wait_ge(f["f_xT_ps"], g + 1)
                    if g >= 2:
                        act.wait_ge(f["f_p_ps"], g - 1)
                    nc.scalar.activation(xnT2[:, j, :], work[FFN_BANK["xT"]][:], ACT.Copy).then_inc(f["f_xT"], 1)
                elif stage == "p":
                    act.wait_ge(f["f_p_ps"], g + 1)
                    if g >= 2:
                        act.wait_ge(f["f_h_ps"], (g - 1) * (FF // P))
                    nc.scalar.activation(pT[j], work[FFN_BANK["p"]][0:SPLIT, :], ACT.Copy).then_inc(f["f_p"], 1)
                elif stage == "h":
                    for k in range(FF // P):
                        act.wait_ge(f["f_h_ps"], g * (FF // P) + k + 1)
                        if g >= 1 and k == 0:
                            act.wait_ge(f["f_q_ps"], g)
                        if g == 0 and k == 0:
                            act.wait_ge(s["pv_done"], at(u, PV_N, 0))
                        nc.scalar.activation(hT[:, k, :], work[FFN_BANK[f"h{k}"]][:], ACT.Gelu_apprx_tanh,
                                             bias=b1c[:, k:k + 1]).then_inc(f["f_h"], 1)
                else:
                    act.wait_ge(f["f_q_ps"], g + 1)
                    if g >= 2:
                        act.wait_ge(f["f_z_ps"], g - 1)
                    nc.scalar.activation(q_parts[:, j, :], work[FFN_BANK["q"]][:], ACT.Copy).then_inc(f["f_q"], 1)

        def dve_max(dve, v, r):
            for h in range(2):
                c, qt, kc = r // (TC * NC), r // NC % TC, r % NC
                dve.wait_ge(s["max_ready"], at(v, MAXN, 2 * r + h + 1))
                if qt == 0 and kc == 0 and h == 0 and not (is_first(v) and c < 2):
                    dve.wait_ge(s["neg_max_done"], at(v, NC, c - 1))
                nc.vector.reduce_max(max_part[:, c % 2, h * TC + qt, kc:kc + 1], work[BANK["max", 2 * r + h]][:],
                                     AX.X).then_inc(s["max_done"], 1)

        def dve_neg_max(dve, v, c):
            dve.wait_ge(s["max_done"], at(v, MAXN, 2 * TC * NC * (c + 1)))
            if not (is_first(v) and c < 2):
                dve.wait_ge(s["m_ps"], at(v, NC, c - 1))
            nc.vector.tensor_reduce(neg_max[:, c % 2, :], max_part[:, c % 2, :, :], AX.X, ALU.max,
                                    negate=True).then_inc(s["neg_max_done"], 1)

        def dve_v(dve, v, c, before_v):
            b = v[1]
            dve.wait_ge(s["v_ps"], at(v, NC, c + 1))
            if c == 0 and before_v is not None:
                dve.wait_ge(s["pv_done"], at(before_v, PV_N, PV_N))
            nc.vector.tensor_tensor(v_sb[b][:, c * TC:(c + 1) * TC, :],
                                    work[BANK["V", c]][:].rearrange("p (t n) -> p t n", t=TC),
                                    b_v[:].unsqueeze(1).to_broadcast([P, TC, P]), ALU.add).then_inc(s["v_done"], 1)

        def dve_tail(dve, u, c, kt, last=False):
            if kt == SUM_AT:
                dve.wait_ge(s["dve_sum_done"], at(u, DVE_SUM_N, (c + 1) * DVE_ADDS))
                dve.wait_ge(s["pool_sum_done"], at(u, POOL_SUM_N, (c + 1) * POOL_ADDS))
                if not (is_first(u) and c == 0):
                    dve.wait_ge(s["denom_ps_ready"], at(u, NC, c))
                nc.vector.tensor_tensor(sum_all[:], dve_sum[:], pool_sum[:], ALU.add).then_inc(s["sum_all_done"], 1)
            if kt == RECIP_AT:
                dve.wait_ge(s["col_dma"], at(u, TAIL_DMA_N, 2 * 16 * (c + 1)))
                nc.vector.reciprocal(denom_col[:], denom_col[:]).then_inc(s["recip_done"], 1)
            if kt == NORM_AT:
                if last:
                    dve.wait_ge(s["denom_copied"], at(u, NC, NC))
                else:
                    dve.wait_ge(s["denom_dma"], at(u, TAIL_DMA_N, 2 * 16 * (c + 1)))
                dve.wait_ge(s["pv_done"], at(u, PV_N, (c + 1) * T))
                if not (is_first(u) and c == 0):
                    dve.wait_ge(s["wo_ps_ready"], at(u, NC, c))
                nc.vector.tensor_tensor(o_norm[:], o_ps[c % 2][:], denom[:], ALU.mult).then_inc(s["o_norm_done"], 1)
            if kt == Y_AT:
                b = u[1]
                dve.wait_ge(s["wo_ps_ready"], at(u, NC, c + 1))
                part = y_acc[:, b * T + c * TC:b * T + (c + 1) * TC, :]
                nc.vector.tensor_tensor(part, work[BANK["Wo", c]][:].rearrange("p (t n) -> p t n", t=TC), part,
                                        ALU.add).then_inc(s["y_done"], 1)

        def add_tile(eng, u, st, tiles, done, total):
            c, kt = st // T, st % T
            k, adds = tiles.index(kt), len(tiles) - 1
            if k == 0:
                return
            eng.wait_ge(s["exp_done"], at(u, SCORE_N, 2 * st + 2))
            if k == 1:
                if not (is_first(u) and c == 0):
                    eng.wait_ge(s["sum_all_done"], at(u, NC, c))
                so_far = probs[:, (st - kt + tiles[0]) % PRING, :, :]
            else:
                eng.wait_ge(done, at(u, NC * adds, c * adds + k - 1))
                so_far = total[:]
            eng.tensor_tensor(total[:], so_far, probs[:, st % PRING, :, :], ALU.add).then_inc(done, 1)

        def dve_unit(dve, u, before, last=False):
            v = following(u)
            for st in range(STEPS):
                c, kt = st // T, st % T
                done = (u, c - 1) if c else (before, NC - 1)
                if kt == Y_AT and done[0] is not None:
                    dve_tail(dve, *done, kt)
                for r, who in step_pairs(st, is_first(u)):
                    if who == "this" or not last:
                        dve_max(dve, u if who == "this" else v, r)
                for kind, pc, who in step_preps(st, is_first(u)):
                    if kind == "V" and not last:
                        dve_v(dve, v, pc, before)
                for kind, pc, who in step_preps(st + 1, is_first(u)):
                    if kind == "M" and (who == "this" or not last):
                        dve_neg_max(dve, u if who == "this" else v, pc)
                if kt in (SUM_AT, RECIP_AT, NORM_AT) and done[0] is not None:
                    dve_tail(dve, *done, kt)
                if st and (st - 1) % T in DVE_TILES:
                    add_tile(dve, u, st - 1, DVE_TILES, s["dve_sum_done"], dve_sum)
                elif st == 0 and before is not None and T - 1 in DVE_TILES:
                    add_tile(dve, before, STEPS - 1, DVE_TILES, s["dve_sum_done"], dve_sum)
                if last:
                    dve_ffn(dve, u, st)
            if last:
                add_tile(dve, u, STEPS - 1, DVE_TILES, s["dve_sum_done"], dve_sum)
                for st in range(STEPS, LAST_STEPS):
                    if st == END_SUM:
                        dve_tail(dve, u, NC - 1, SUM_AT)
                    if st == END_DENOM:
                        dve.wait_ge(s["denom_ps_ready"], at(u, NC, NC))
                        dve.wait_ge(s["o_norm_done"], at(u, NC, NC - 1))
                        nc.vector.reciprocal(denom[:], work[BANK["L", NC - 1]][:]).then_inc(s["denom_copied"], 1)
                    if st == END_NORM:
                        dve_tail(dve, u, NC - 1, NORM_AT, last=True)
                    if st == END_Y:
                        dve_tail(dve, u, NC - 1, Y_AT)
                    dve_ffn(dve, u, st)

        def statistics(dve, tiles, slot, stats_sem, mv_sem, n):
            for t in range(TC):
                ins = nc.vector.bn_stats(ln_stats[:, slot, t, :], tiles[t])
            ins.then_inc(stats_sem, 1)
            dve.wait_ge(stats_sem, n + 1)
            for t in range(TC):
                ins = nc.vector.bn_aggr(ln_mv[:, slot, t, :], ln_stats[:, slot, t, :])
            ins.then_inc(mv_sem, 1)

        def normalise(dve, tiles, outs, slot, mv_sem, rstd_sem, out_sem, n):
            dve.wait_ge(mv_sem, n + 1)
            dve.wait_ge(rstd_sem, n + 1)
            for t in range(TC):
                nc.vector.tensor_scalar(outs[t], tiles[t], ln_mv[:, slot, t, 0:1], ln_rstd[:, slot, t:t + 1],
                                        ALU.subtract, ALU.mult).then_inc(out_sem, 1)

        def dve_ffn(dve, u, st):
            for stage, g in ffn_at(st, "norm1", "x1", "norm2", "low", "norm3", "out"):
                j = g % 2
                x1 = y_acc[:, g * TC:(g + 1) * TC, :]
                x1_t = [x1[:, t, :] for t in range(TC)]
                xn_t = [xn[:, j, t, :] for t in range(TC)]
                z_t = [z[j][:, t, :] for t in range(TC)]
                if stage == "norm1":
                    dve.wait_ge(s["y_done"], at((PAIRS - 1, g // NC), NC, g % NC + 1))
                    statistics(dve, x1_t, 2, f["f_st1"], f["f_mv1"], g)
                elif stage == "x1":
                    normalise(dve, x1_t, x1_t, 2, f["f_mv1"], f["f_rs1"], f["f_yn"], g)
                    dve.wait_ge(f["f_yn"], TC * (g + 1))
                    dve.wait_ge(g_in[j], 16 * (g // 2 + 1))
                    nc.vector.tensor_tensor(x1, x1, xg[:, j], ALU.add).then_inc(f["f_x1"], 1)
                    dve.wait_ge(f["f_x1"], g + 1)
                    statistics(dve, x1_t, 0, f["f_st2"], f["f_mv2"], g)
                elif stage == "norm2":
                    if g == 0:
                        dve.wait_ge(s["score_ready"], at(u, SCORE_N, 0))
                    if g >= 2:
                        dve.wait_ge(f["f_xT_ps"], g - 1)
                    normalise(dve, x1_t, xn_t, 0, f["f_mv2"], f["f_rs2"], f["f_xn"], g)
                elif stage == "low":
                    if g == 0:
                        dve.wait_ge(f["v1_high"], 1)
                        nc.vector.tensor_tensor(v1_third, v1_f32[2 * RANK:SPLIT], v1_third.bitcast(F32),
                                                ALU.subtract).then_inc(f["v1_split"], 2)
                    dve.wait_ge(f["f_p"], g + 1)
                    nc.vector.tensor_tensor(pT_low[j], work[FFN_BANK["p"]][RANK:2 * RANK, :], pT_low[j].bitcast(F32),
                                            ALU.subtract).then_inc(f["f_low"], 1)
                elif stage == "norm3":
                    dve.wait_ge(f["f_z_ps"], g + 1)
                    if g == 0:
                        dve.wait_ge(f["ffn_w_in"], FFN_W_N)
                        dve.wait_ge(s["kq_split"], at(u, KQ_N, KQ_N))
                    if g >= 2:
                        dve.wait_ge(out_dma[j], 16 * (g // 2))
                    nc.vector.tensor_tensor(z[j], work[FFN_BANK["z"]][:].rearrange("p (t d) -> p t d", t=TC),
                                            b2r[:].unsqueeze(1).to_broadcast([P, TC, D]), ALU.add).then_inc(f["f_z"], 1)
                    dve.wait_ge(f["f_z"], g + 1)
                    statistics(dve, z_t, 1, f["f_st3"], f["f_mv3"], g)
                else:
                    normalise(dve, z_t, z_t, 1, f["f_mv3"], f["f_rs3"], f["f_zn"], g)
                    dve.wait_ge(f["f_zn"], TC * (g + 1))
                    nc.vector.tensor_tensor(z[j], z[j], x1, ALU.add).then_inc(f["f_out"], 1)

        def pool_split(pool, v, kind, c):
            n = c + (NC if kind == "Q" else 0)
            hi, lo = (k_hi, k_lo) if kind == "K" else (q_hi, q_lo)
            pool.wait_ge(s["kq_evac"], at(v, KQ_N, n + 1))
            nc.gpsimd.tensor_tensor(lo[:, c % 2, :], kq_f32[:, n % 2, :], hi[:, c % 2, :].bitcast(F32),
                                    ALU.subtract).then_inc(s["kq_split"], 1)

        def pool_unit(pool, u, before, last=False):
            v = following(u)
            for st in range(STEPS):
                kt = st % T
                for kind, pc, who in step_preps(st, is_first(u)):
                    if kind in "KQ" and (who == "this" or not last):
                        pool_split(pool, u if who == "this" else v, kind, pc)
                if last:
                    pool_ffn(pool, st)
                if kt in POOL_TILES:
                    add_tile(pool, u, st, POOL_TILES, s["pool_sum_done"], pool_sum)
            if last:
                for st in range(STEPS, LAST_STEPS):
                    pool_ffn(pool, st)

        def inverse_deviation(pool, slot, mv_ready, added, rstd_ready, n):
            pool.wait_ge(mv_ready, n + 1)
            nc.gpsimd.tensor_scalar(ln_var[:, slot, :], ln_mv[:, slot, :, 1], EPS, None, ALU.add).then_inc(added, 1)
            pool.wait_ge(added, n + 1)
            nc.gpsimd.tensor_tensor(ln_rstd[:, slot, :], ln_var[:, slot, :], minus_half[:],
                                    ALU.pow).then_inc(rstd_ready, 1)

        def pool_ffn(pool, st):
            for stage, g in ffn_at(st, "norm1", "x1", "norm3"):
                k, slot = {"norm1": (1, 2), "x1": (2, 0), "norm3": (3, 1)}[stage]
                inverse_deviation(pool, slot, f[f"f_mv{k}"], f[f"f_ep{k}"], f[f"f_rs{k}"], g)

        def sp_weights(sp, i):
            for dst, src in ((w_qkv[:, 0, :], wq_v[i]), (w_qkv[:, 1, :], wk_v[i]), (w_qkv[:, 2, :], wv_v[i]),
                             (b_qk[:, 0:1], bq_v[i].unsqueeze(1)), (b_qk[:, 1:2], bk_v[i].unsqueeze(1)),
                             (b_v[:], bv_v[i].partition_broadcast(P))):
                sp.dma_start(dst, src).then_inc(s["w_in"], 16)

        def sp_k(sp, v, c, free_after=None):
            b = v[1]
            split, read = at(v, KQ_N, c + 1), free_after and at(free_after, SCORE_N, 0)
            sp.wait_ge(s["kq_split"], split)
            if free_after is not None:
                sp.wait_ge(s["score_ready"], read)
            cols, j = slice(c * CH, (c + 1) * CH), c % 2
            for h in range(2):
                rows = slice(h * HD, (h + 1) * HD)
                sp.dma_start(k_dup[b][0:HD, h, cols].bitcast(F32), k_hi[rows, j, :].bitcast(F32)).then_inc(k_dma[j], 16)
                sp.dma_start(k_dup[b][HD:P, h, cols].bitcast(F32), k_hi[rows, j, :].bitcast(F32)).then_inc(k_dma[j], 16)
                sp.dma_start(k_low[b][0:HD, h, cols].bitcast(F32), k_lo[rows, j, :].bitcast(F32)).then_inc(k_dma[j], 16)

        def sp_q(sp, v, c, u):
            split, read = at(v, KQ_N, NC + c + 1), u and at(u, SCORE_N, 2 * T * (c + 1))
            sp.wait_ge(s["kq_split"], split)
            if u is not None:
                sp.wait_ge(s["score_ready"], read)
            cols, j = slice(c * CH, (c + 1) * CH), c % 2
            for h in range(2):
                rows = slice(h * HD, (h + 1) * HD)
                sp.dma_start(q_split[0:HD, h, cols].bitcast(F32), q_hi[rows, j, :].bitcast(F32)).then_inc(q_dma[j], 16)
                sp.dma_start(q_split[HD:P, h, cols].bitcast(F32), q_lo[rows, j, :].bitcast(F32)).then_inc(q_dma[j], 16)
                sp.dma_start(q_max[0:HD, h, cols].bitcast(F32), q_hi[rows, j, :].bitcast(F32)).then_inc(q_dma[j], 16)

        def sp_denom(sp, u, c):
            sp_denom_out(sp, u, c)
            sp_denom_back(sp, u, c)

        def sp_denom_out(sp, u, c):
            sp.wait_ge(s["denom_copied"], at(u, NC, c + 1))
            for h in range(2):
                rows = slice(h * HD, (h + 1) * HD)
                sp.dma_start(denom_col[rows, :], denom[h * HD:h * HD + 1, :]).then_inc(s["col_dma"], 16)

        def sp_denom_back(sp, u, c):
            sp.wait_ge(s["recip_done"], at(u, NC, c + 1))
            sp.dma_start(denom_dram.rearrange("h (p n) -> (h p) n", p=HD), denom_col[:]).then_inc(s["scratch_dma"], 16)
            sp.wait_ge(s["scratch_dma"], at(u, NC * 16, 16 * (c + 1)))
            for h in range(2):
                sp.dma_start(denom[h * HD:(h + 1) * HD, :],
                             denom_dram[h].partition_broadcast(HD)).then_inc(s["denom_dma"], 16)

        def sp_m(sp, v, c):
            sp.wait_ge(s["m_evac"], at(v, NC, c + 1))
            for h in range(2):
                dst = q_max[HD:HD + 1, h, c * CH:(c + 1) * CH].bitcast(F32).rearrange("o (t n) -> o t n", t=TC)
                sp.dma_start(dst, max_rows[h * TC:(h + 1) * TC, c % 2, :].bitcast(F32)).then_inc(m_dma[c % 2], 16)

        def sp_ffn_weights(sp, u):
            sp.wait_ge(s["score_ready"], at(u, SCORE_N, 0))
            thirds = [slice(k * RANK, (k + 1) * RANK) for k in range(3)]
            loads = [(u1[:, k], U1) for k in thirds] + [(v1_f32[k, :], V1) for k in thirds]
            loads += [(b1c[:], b1.rearrange("(f p) -> p f", p=P)), (u2[:], U2.rearrange("(f p) r -> p f r", p=P))]
            loads += [(v2[k * RANK:(k + 1) * RANK, :], V2) for k in range(FF // P)]
            loads += [(b2r[:], b2.partition_broadcast(P))]
            assert 16 * len(loads) == FFN_W_N
            for dst, src in loads:
                sp.dma_start(dst, src, allow_slow_non_contiguous=src.shape[0] == P and src.shape[-1] == FF // P).then_inc(f["ffn_w_in"], 16)

        def sp_x(sp, g):
            if g == 0:
                sp.wait_ge(s["xnT_ps_ready"], NG)
            if g >= 2:
                sp.wait_ge(f["f_x1"], g - 1)
            sp.dma_start(xg[:, g % 2], x_v[:, g * TC:(g + 1) * TC, :]).then_inc(g_in[g % 2], 16)

        def sp_out(sp, g):
            sp.wait_ge(f["f_out"], g + 1)
            sp.dma_start(out_v[:, g * TC:(g + 1) * TC, :], z[g % 2]).then_inc(out_dma[g % 2], 16)

        def sp_next_weights(sp, u, v):
            projected, evacuated, v_done = at(v, NC, NC), at(v, KQ_N, KQ_N), at(v, NC, NC)
            sp.wait_ge(s["q_ps"], projected)
            sp.wait_ge(s["kq_evac"], evacuated)
            sp.wait_ge(s["v_done"], v_done)
            if not isinstance(u[0], int) or u[0] < PAIRS - 1:
                sp_weights(sp, number(u[0]) + 1)

        def sp_unit(sp, u, before, last=False):
            v = following(u)
            if last:
                sp_ffn_weights(sp, u)
                events = [(M_LATE, sp_m, (u, NC - 1))]
                for w, c in [(before, NC - 1)] + [(u, c) for c in range(NC - 1)]:
                    chunk_end = 0 if w is before else (c + 1) * T
                    events += [(chunk_end + DENOM_AT, sp_denom_out, (w, c)), (chunk_end + RECIP_AT, sp_denom_back, (w, c))]
                events += [(GROUP_AT[g] - 3, sp_x, (g,)) for g in range(NG)]
                events += [(GROUP_AT[g] + FFN_AT["out"] + 1, sp_out, (g,)) for g in range(NG)]
                for _, send, what in sorted(events, key=lambda event: event[0]):
                    send(sp, *what)
                for j in range(2):
                    sp.wait_ge(out_dma[j], 16 * (NG // 2))
                return
            if is_first(u):
                events = [(OWN_Q_AT[c] + 1, sp_q, (u, c, None)) for c in range(1, NC)]
                events += [(OWN_M_AT[c] + 1, sp_m, (u, c)) for c in range(1, NC)]
                events += [(FIRST_K_AT[c] + 1, sp_k, (v, c)) for c in range(NC)]
                events += [((c + 1) * T + DENOM_AT, sp_denom_out, (u, c)) for c in range(NC - 1)]
                events += [((c + 1) * T + RECIP_AT, sp_denom_back, (u, c)) for c in range(NC - 1)]
                events += [(max(FIRST_Q_AT[c] + 1, (c + 1) * T), sp_q, (v, c, u)) for c in range(NC)]
                events += [(FIRST_M_AT[c] + 1, sp_m, (v, c)) for c in range(NC - 1)]
                events += [(STEPS - 1, sp_next_weights, (u, v))]
                for _, send, what in sorted(events, key=lambda event: event[0]):
                    send(sp, *what)
                return
            sp_k(sp, v, 0, free_after=None if before is None else u)
            sp_k(sp, v, 1)
            sp_m(sp, u, NC - 1)
            sp_k(sp, v, 2)
            sp_k(sp, v, 3)
            if before is not None:
                sp_denom(sp, before, NC - 1)
            if u[1] == 0 and before is not None:
                sp.wait_ge(s["wo_ps_ready"], at(u, NC, 0))
                sp.dma_start(w_o[:], wo_v[number(u[0])]).then_inc(s["wo_in"], 16)
            for c in range(NC):
                if c == NC - 1 and u[1] == 0:
                    sp_next_weights(sp, u, v)
                sp_q(sp, v, c, u)
                if c < NC - 1:
                    sp_denom(sp, u, c)
                    sp_m(sp, v, c)

        def units(name, eng, unit_fn):
            unit_fn(eng, (0, 0), None)
            unit_fn(eng, (0, 1), (0, 0))
            base = {n: eng.alloc_register(f"{name}_after_{n}") for n in UNIT_COUNTS}
            spare = [eng.alloc_register(f"{name}_wait_value{k}") for k in range(4)]
            for n, r in base.items():
                eng.reg_mov(r, B * n)
            with eng.Fori(1, PAIRS - 1) as number:
                i = Pair(eng, number, base, spare)
                unit_fn(eng, (i, 0), (i - 1, 1))
                unit_fn(eng, (i, 1), (i, 0))
                for n, r in base.items():
                    eng.reg_add(r, r, B * n)
            n = PAIRS - 1
            unit_fn(eng, (n, 0), (n - 1, 1))
            unit_fn(eng, (n, 1), (n, 0), last=True)

        first_xn = probs[:].rearrange("p r h n -> p r (h n)")[:, :, 0:CH].rearrange("p r (t d) -> p r t d", t=TC)

        f_names = """v1_high v1_split f_low f_ep1 f_ep2 f_ep3 ffn_w_in g_in0 g_in1 f_st1 f_mv1 f_rs1 f_yn f_x1 f_st2 f_mv2 f_rs2 f_xn f_xT_ps f_xT f_p_ps f_p
            f_h_ps f_h f_q_ps f_q f_z_ps f_z f_st3 f_mv3 f_rs3 f_zn f_out out_dma0 out_dma1""".split()
        f = {n: sem(n) for n in f_names}
        g_in = [f["g_in0"], f["g_in1"]]
        out_dma = [f["out_dma0"], f["out_dma1"]]
        FFN_W_N = 16 * (3 + 3 + 1 + 1 + FF // P + 1)
        v1_third = v1_split[2 * RANK:SPLIT, :]
        pT = [p_split[:, j, :] for j in range(2)]
        pT_low = [p_split[RANK:2 * RANK, j, :] for j in range(2)]
        hT = v_sb[0][:].rearrange("p t n -> p (t n)").rearrange("p (f n) -> p f n", f=FF // P)
        z = [kq_f32[:, j, :].rearrange("p (t d) -> p t d", t=TC) for j in range(2)]

        late_x = [first_xn[:, 2 + j] for j in range(2)]

        block = ctx.enter_context(nc.Block())

        @block.sync
        def _(sp):
            for g in range(NG - 2):
                if g >= 2:
                    sp.wait_ge(s["xn_done"], TC * (g - 1))
                sp.dma_start(xg[:, g % 2], x_v[:, g * TC:(g + 1) * TC, :]).then_inc(s[f"x_in{g % 2}"], 16)
                if g == 1:
                    for j in range(2):
                        sp.dma_start(late_x[j], x_v[:, (NG - 2 + j) * TC:(NG - 1 + j) * TC, :]).then_inc(s[f"x_late{j}"], 16)
                    sp_weights(sp, 0)
                    sp.dma_start(w_o[:], wo_v[0]).then_inc(s["wo_in"], 16)
                    sp.dma_start(y_acc[:, 0, :], bo.partition_broadcast(P)).then_inc(s["y_init"], 16)
            first = (0, 0)
            for c in range(NC):
                sp_k(sp, first, c)
            sp_q(sp, first, 0, None)
            sp_m(sp, first, 0)
            units("sp", sp, sp_unit)

        @block.gpsimd
        def _(pool):
            nc.gpsimd.memset(minus_half[:], -0.5).then_inc(s["half_ready"], 1)
            pool.wait_ge(s["half_ready"], 1)
            nc.gpsimd.memset(ident[:], 0.0).then_inc(s["const_ready"], 1)
            pool.wait_ge(s["const_ready"], 1)
            nc.gpsimd.affine_select(out=ident[:], in_=ident[:], compare_op=ALU.not_equal, fill=1.0, base=0,
                                    pattern=[[-1, P]], channel_multiplier=1).then_inc(s["const_ready"], 1)
            nc.gpsimd.memset(ones[:], 1.0).then_inc(s["const_ready"], 1)
            pool.wait_ge(s["const_ready"], 3)
            for b in range(B):
                if b:
                    pool.wait_ge(s["ones_row"], b)
                nc.gpsimd.memset(k_low[b][HD:HD + 1, :, :].bitcast(F32), 1.0).then_inc(s["ones_row"], 1)
            pool.wait_ge(s["ones_row"], B)
            for what, g in START_POOL:
                if what == "K":
                    pool_split(pool, (0, 0), "K", g)
                else:
                    inverse_deviation(pool, g % 2, s["mv_done"], s["eps_added"], s["rstd_done"], g)
            pool_split(pool, (0, 0), "Q", 0)
            units("pool", pool, pool_unit)

        @block.scalar
        def _(act):
            for what, g in START:
                if what == "K":
                    act_evac(act, (0, 0), "K", g)
                    continue
                act.wait_ge(s["xnT_ps_ready"], g + 1)
                nc.scalar.activation(xnT[:, g * CH:(g + 1) * CH], o_ps[g % 2][:], ACT.Copy).then_inc(s["xnT_done"], 1)
                if g == 1:
                    act.wait_ge(s["y_init"], 16)
                    nc.scalar.activation(y_acc[:, 1:B * T, :], y_acc[:, 0:1, :].to_broadcast([P, B * T - 1, D]),
                                         ACT.Copy).then_inc(s["y_init"], 1)
            first = (0, 0)
            act_evac(act, first, "Q", 0)
            act_evac(act, first, "M", 0)
            units("act", act, act_unit)

        @block.vector
        def _(dve):
            for g in range(NG):
                j = g % 2
                if g < NG - 2:
                    dve.wait_ge(s[f"x_in{j}"], 16 * (g // 2 + 1))
                else:
                    dve.wait_ge(s[f"x_late{j}"], 16)
                if g >= 2:
                    dve.wait_ge(s["xnT_ps_ready"], g - 1)
                x_t = [(xg[:, j] if g < NG - 2 else late_x[j])[:, t, :] for t in range(TC)]
                xn_t = [first_xn[:, j, t, :] for t in range(TC)]
                statistics(dve, x_t, j, s["stats_done"], s["mv_done"], g)
                normalise(dve, x_t, xn_t, j, s["mv_done"], s["rstd_done"], s["xn_done"], g)
            first = (0, 0)
            for _, kind, c in PREP:
                if kind == "V":
                    dve_v(dve, first, c, None)
            for r in range(TC * NC):
                dve_max(dve, first, r)
            dve_neg_max(dve, first, 0)
            dve.wait_ge(s["y_init"], 17)
            units("dve", dve, dve_unit)

        @block.tensor
        def _(pe):
            pe.wait_ge(s["const_ready"], 3)
            me = Pe(pe)
            for what, g in START:
                if what == "K":
                    pe.wait_ge(s["xnT_done"], NC)
                    me.project((0, 0), "K", g)
                    continue
                pe.wait_ge(s["xn_done"], TC * (g + 1))
                if g >= 2:
                    pe.wait_ge(s["xnT_done"], g - 1)
                for t in range(TC):
                    last = nc.tensor.transpose(o_ps[g % 2][:, t * P:(t + 1) * P], first_xn[:, g % 2, t, :], ident[:])
                last.then_inc(s["xnT_ps_ready"], 1)
            pe.wait_ge(s["xnT_done"], NG)
            me.prepare_alone((0, 0))
            units("pe", pe, lambda _, u, before, last=False: me.unit(u, before, last))

_INS = ['L0_attn_x', 'L0_attn_Wq', 'L0_attn_bq', 'L0_attn_Wk', 'L0_attn_bk', 'L0_attn_Wv', 'L0_attn_bv',
        'L0_attn_Wo', 'L0_attn_bo', 'L0_ffn_U1', 'L0_ffn_V1', 'L0_ffn_b1', 'L0_ffn_U2', 'L0_ffn_V2', 'L0_ffn_b2']


def kernel(**inputs):
    import numpy as _np
    import concourse.bacc as _bacc
    from concourse import mybir as _mybir
    from concourse.bass_utils import run_bass_kernel_spmd as _run

    nc = _bacc.Bacc("TRN2", target_bir_lowering=False, num_devices=1)
    arrays, args = {}, []
    for name in _INS:
        a = _np.ascontiguousarray(inputs[name])
        arrays[f"in_{name}"] = a
        args.append(nc.dram_tensor(f"in_{name}", a.shape, _mybir.dt.from_np(a.dtype), kind="ExternalInput").ap())
    x = arrays["in_L0_attn_x"]
    args.append(nc.dram_tensor("block_out", x.shape, _mybir.dt.from_np(x.dtype), kind="ExternalOutput").ap())
    build(nc, *args)
    return _run(nc, [arrays], core_ids=[0]).results[0]["block_out"]
```
